# Optimizing a Trainium2 kernel written in Bass

```python
import numpy as np
import jax
import jax.numpy as jnp

def _softmax(x, axis=-1):
    return jax.nn.softmax(x, axis=axis)

def _gelu(x):
    return jax.nn.gelu(x, approximate=True)

def _silu(x):
    return jax.nn.silu(x)

def _sigmoid(x):
    return jax.nn.sigmoid(x)

def _layernorm(x, axis=-1, eps=1e-05):
    m = jnp.mean(x, axis=axis, keepdims=True)
    v = jnp.var(x, axis=axis, keepdims=True)
    return (x - m) / jnp.sqrt(v + eps)

def _scatter_add(tgt, idx, src, axis=0):
    return tgt.at[idx].add(src)

def _segment_sum(src, seg, n):
    return jax.ops.segment_sum(src, seg, n)
kernel_name = 'mk_adj_preln_d2_adj_r2_3ed6f8'

def setup_inputs(seed: int=0):
    np.random.seed(seed)
    _w = jnp.asarray

    def _rec_inputs():
        import jax
        import jax.numpy as jnp
        _gk = jax.random.key(seed)
        x = -0.0003929 + 0.9999 * jax.random.normal(jax.random.fold_in(_gk, 1), (32, 256, 512), jnp.float32)
        _a = jax.random.bernoulli(jax.random.fold_in(_gk, 2), 0.0078125, (256, 256))
        _a = jnp.logical_or(_a, jnp.swapaxes(_a, -1, -2))
        _a = jnp.logical_or(_a, jnp.eye(256, dtype=bool))
        _af = _a.astype(jnp.float32)
        _af = _af * jax.random.uniform(jax.random.fold_in(_gk, 3), (256, 256), jnp.float32, 0.05, 0.198159)
        adj = _af
        return (x, adj)
    x, adj = _rec_inputs()

    def _L0_gnn_setup():
        import jax, jax.numpy as jnp
        import numpy as np
        NEG_SLOPE = 0.01
        key = jax.random.key(seed)
        k1, k2, k3, k4, k5 = jax.random.split(key, 5)
        B, C, N, O = (32, 256, 512, 256)
        x = jax.random.normal(k1, (B, C, N), dtype=jnp.float32)
        wq = jax.random.normal(k2, (C,), dtype=jnp.float32) * (1.0 / np.sqrt(C))
        wk = jax.random.normal(k3, (C,), dtype=jnp.float32) * (1.0 / np.sqrt(C))
        wm = jax.random.normal(k4, (O, C), dtype=jnp.float32) * (1.0 / np.sqrt(C))
        bm = jax.random.normal(k5, (O,), dtype=jnp.float32) * 0.01
        return {'x': x, 'wq': wq, 'wk': wk, 'wm': wm, 'bm': bm}
    _L0_gnn_all = _L0_gnn_setup()
    _L0_gnn_in = {k: v for k, v in _L0_gnn_all.items() if k in ('wq', 'wk', 'bm')}
    del _L0_gnn_all

    def _L1_gnn_setup():
        import jax, jax.numpy as jnp
        import numpy as np
        EPS = 1e-08

        def _row_stochastic_causal(A, causal_mask):
            A = A * causal_mask
            deg = jnp.maximum(A.sum(axis=-1, keepdims=True), EPS)
            return A / deg
        key = jax.random.key(seed)
        k = jax.random.split(key, 5)
        B, N, D = (4, 1024, 512)
        s = 1.0 / np.sqrt(D)
        h = jax.random.normal(k[0], (B, N, D), dtype=jnp.float32)
        W_lang = jax.random.normal(k[1], (D, D), dtype=jnp.float32) * s
        W_grav = jax.random.normal(k[2], (D, D), dtype=jnp.float32) * s
        W_V = jax.random.normal(k[3], (D, D), dtype=jnp.float32) * s
        W_O = jax.random.normal(k[4], (D, D), dtype=jnp.float32) * s
        causal_mask = jnp.tril(jnp.ones((N, N), dtype=jnp.float32))
        gate_logit = jnp.zeros((), jnp.float32)
        log_sigma = jnp.zeros((), jnp.float32)
        return {'h': h, 'causal_mask': causal_mask, 'W_lang': W_lang, 'W_grav': W_grav, 'W_V': W_V, 'W_O': W_O, 'gate_logit': gate_logit, 'log_sigma': log_sigma}
    _L1_gnn_all = _L1_gnn_setup()
    _L1_gnn_in = {k: v for k, v in _L1_gnn_all.items() if k in ('W_lang', 'W_grav', 'W_V', 'W_O', 'gate_logit', 'log_sigma')}
    del _L1_gnn_all
    return {'x': x, 'adj': adj, 'L0_gnn_wq': _L0_gnn_in['wq'], 'L0_gnn_wk': _L0_gnn_in['wk'], 'L0_gnn_bm': _L0_gnn_in['bm'], 'L1_gnn_W_lang': _L1_gnn_in['W_lang'], 'L1_gnn_W_grav': _L1_gnn_in['W_grav'], 'L1_gnn_W_V': _L1_gnn_in['W_V'], 'L1_gnn_W_O': _L1_gnn_in['W_O'], 'L1_gnn_gate_logit': _L1_gnn_in['gate_logit'], 'L1_gnn_log_sigma': _L1_gnn_in['log_sigma']}

def reference(x, adj, L0_gnn_wq, L0_gnn_wk, L0_gnn_bm, L1_gnn_W_lang, L1_gnn_W_grav, L1_gnn_W_V, L1_gnn_W_O, L1_gnn_gate_logit, L1_gnn_log_sigma):
    import jax
    import jax.numpy as jnp

    def _L0_gnn_ref(x, wq, wk, wm, bm):
        import jax, jax.numpy as jnp
        import numpy as np
        NEG_SLOPE = 0.01
        q = jnp.einsum('c,bcn->bn', wq, x)
        k = jnp.einsum('c,bcn->bn', wk, x)
        scores = q[:, None, :] + k[:, :, None]
        scores = jnp.where(scores > 0, scores, NEG_SLOPE * scores)
        att = jax.nn.softmax(scores, axis=-1)
        agg = jnp.einsum('bcn,bmn->bcm', x, att)
        out = jnp.einsum('oc,bcm->bom', wm, agg) + bm[None, :, None]
        return jax.nn.relu(out)

    def _L1_gnn_ref(h, causal_mask, W_lang, W_grav, W_V, W_O, gate_logit, log_sigma):
        import jax, jax.numpy as jnp
        import numpy as np
        EPS = 1e-08

        def _row_stochastic_causal(A, causal_mask):
            A = A * causal_mask
            deg = jnp.maximum(A.sum(axis=-1, keepdims=True), EPS)
            return A / deg
        z_l = jnp.einsum('bnd,ed->bne', h, W_lang)
        z_g = jnp.einsum('bnd,ed->bne', h, W_grav)
        v = jnp.einsum('bnd,ed->bne', h, W_V)
        N = h.shape[-2]
        not_eye = 1.0 - jnp.eye(N, dtype=h.dtype)
        zn = z_l / jnp.maximum(jnp.linalg.norm(z_l, axis=-1, keepdims=True), EPS)
        A_l = jnp.maximum(jnp.einsum('bnd,bmd->bnm', zn, zn), 0.0) * not_eye
        sq = jnp.sum(z_g * z_g, axis=-1, keepdims=True)
        d2 = jnp.maximum(sq + jnp.swapaxes(sq, -1, -2) - 2.0 * jnp.einsum('bnd,bmd->bnm', z_g, z_g), 0.0)
        sigma = jnp.exp(log_sigma)
        A_g = jnp.exp(-d2 / (2.0 * sigma * sigma)) * not_eye
        K_l = _row_stochastic_causal(A_l, causal_mask)
        K_g = _row_stochastic_causal(A_g, causal_mask)
        w_l = jax.nn.sigmoid(gate_logit)
        K = w_l * K_l + (1.0 - w_l) * K_g
        out = jnp.einsum('bnm,bmd->bnd', K, v)
        return jnp.einsum('bnd,ed->bne', out, W_O)
    h = jnp.maximum(_layernorm(x, axis=-1), 0.0)
    x = x + _L0_gnn_ref(h, L0_gnn_wq, L0_gnn_wk, adj, L0_gnn_bm)
    h = jnp.maximum(_layernorm(x, axis=-1), 0.0)
    x = x + _L1_gnn_ref(h, adj, L1_gnn_W_lang, L1_gnn_W_grav, L1_gnn_W_V, L1_gnn_W_O, L1_gnn_gate_logit, L1_gnn_log_sigma)
    return x

_drawn_inputs = setup_inputs


def setup_inputs(seed=0):
    import zlib

    import numpy as np

    out = dict(_drawn_inputs(seed))
    spreads = {}
    factors = {'L0_gnn_wq': 8.0, 'L0_gnn_wk': 8.0, 'L0_gnn_bm': 6.229, 'L1_gnn_W_lang': 4.445}
    for name, (base, spread) in spreads.items():
        noise = np.random.default_rng([zlib.crc32(name.encode()), seed]).standard_normal(out[name].shape)
        drawn = base * np.exp(spread * noise) if base else spread * noise
        out[name] = jnp.asarray(drawn.astype(out[name].dtype))
    for name, factor in factors.items():
        out[name] = (out[name] * factor).astype(out[name].dtype)
    return out
```

```python
from contextlib import ExitStack

import concourse.bass as bass
from concourse import mybir

P = 128
F32 = mybir.dt.float32
F32R = mybir.dt.float32r
ALU = mybir.AluOpType
ACT = mybir.ActivationFunctionType
AX_X = mybir.AxisListType.X
RMAX = bass.bass_isa.ReduceOp.max

SLOPE = 0.01
LN_EPS = 1e-5
EPS = 1e-8


def reached(eng, semaphore, count):
    if not (isinstance(count, int) and count <= 0):
        eng.wait_ge(semaphore, count)


def reached_apart(eng, semaphore, count, passed):
    eng.wait_ge(semaphore, count)
    if not isinstance(count, int):
        eng.sem_inc(passed, 1)


def program(nc, x, adj, wq, wk, bm, w_lang, w_grav, w_v, w_o, gate_logit, log_sigma, out):
    B, C, D = x.shape
    CT = C // P
    DT = D // P
    TRI = [max((d + 1) * P, 2 * P) for d in range(DT)]
    assert C == 2 * P and D == 4 * P and B % 2 == 0 and B >= 4

    x_v = x.rearrange("b (t p) d -> b p t d", p=P)
    out_v = out.rearrange("b (t p) d -> b p t d", p=P)

    with ExitStack() as ctx:
        def sb(name, shape, dt=F32):
            return ctx.enter_context(nc.sbuf_tensor(name, shape, dt))

        def sem(name):
            return ctx.enter_context(nc.semaphore(name))

        def sems(name, n):
            return [sem(f"{name}_{k}") for k in range(n)]

        ident = sb("ident", [P, P])
        ones = sb("ones", [P, P])
        minus_half = sb("minus_half", [P, 4])
        adj_rows = sb("adj_rows", [P, CT, C])
        adj_off = sb("adj_off", [P, CT, C])
        wqk = sb("wqk", [P, CT, 2])
        adj_t_hi = sb("adj_t_hi", [P, CT, C + 2], F32R)
        adj_t_lo = sb("adj_t_lo", [P, CT, C + 2], F32R)
        bm_col = sb("bm_col", [P, CT])
        gate = sb("gate", [P, 1])
        sigma = sb("sigma", [P, 1])
        mix = sb("mix", [P, 4])
        neg_rate = sb("neg_rate", [P, 1])
        tri_hi = sb("tri_hi", [P, 2, DT, D], F32R)
        tri_lo = sb("tri_lo", [P, 2, DT, D], F32R)
        wvo_hi = sb("wvo_hi", [P, DT, D], F32R)
        wvo_lo = sb("wvo_lo", [P, DT, D], F32R)

        xs = sb("xs", [P, 2, CT, D])
        x2 = sb("x2", [P, 2, CT, D])
        stats1 = sb("stats1", [P, CT, 6])
        mv1 = sb("mv1", [P, CT, 2])
        var1 = sb("var1", [P, CT])
        rstd1 = sb("rstd1", [P, CT])
        y1 = sb("y1", [P, CT, D])
        h1_hi = sb("h1_hi", [P, CT, D], F32R)
        h1_lo = sb("h1_lo", [P, CT, D], F32R)
        ah_hi = sb("ah_hi", [P, DT, C], F32R)
        ah_lo = sb("ah_lo", [P, DT, C], F32R)
        qk = sb("qk", [P, DT, 2])
        q_part = sb("q_part", [P, 1])
        q_max = sb("q_max", [P, 1])
        q_off = sb("q_off", [P, DT])
        k_pos = sb("k_pos", [P, DT])
        att_a = sb("att_a", [P, DT])
        att_c = sb("att_c", [P, DT])
        att_r = sb("att_r", [P, DT])
        r_diag = sb("r_diag", [P, DT, P])
        r_rows = sb("r_rows", [P, D])
        att = sb("att", [P, DT, D])
        att_hi = sb("att_hi", [P, DT, D], F32R)
        att_lo = sb("att_lo", [P, DT, D], F32R)
        att_sum = sb("att_sum", [P, D])
        inv_sum = sb("inv_sum", [P, D])
        msg = sb("msg", [P, CT, D])
        stats2 = sb("stats2", [P, CT, 6])
        mv2 = sb("mv2", [P, CT, 2])
        var2 = sb("var2", [P, CT])
        rstd2 = sb("rstd2", [P, CT])
        y2 = sb("y2", [P, CT, D])
        ht_hi = sb("ht_hi", [P, DT, C], F32R)
        ht_lo = sb("ht_lo", [P, DT, C], F32R)
        t_hi = sb("t_hi", [P, 2, DT, C], F32R)
        t_lo = sb("t_lo", [P, 2, DT, C], F32R)
        ys = sb("ys", [P, 2, CT, C])
        gram = sb("gram", [P, 2, CT, C])
        diag = sb("diag", [P, 4, P])
        sq = sb("sq", [P, 4])
        cols = sb("cols", [P, 4])
        coef = sb("coef", [P, 4])
        g_bias = sb("g_bias", [P, CT])
        deg = sb("deg", [P, 4])
        lang = sb("lang", [P, CT, C])
        grav = sb("grav", [P, CT, C])
        u_hi = sb("u_hi", [P, CT, D], F32R)
        u_lo = sb("u_lo", [P, CT, D], F32R)
        kt_hi = sb("kt_hi", [P, CT, C], F32R)
        kt_lo = sb("kt_lo", [P, CT, C], F32R)

        bank = ctx.enter_context(nc.psum_tensor("bank", [P, 8, 512], F32))

        w_slot = [att[:, :, :], x2[:, :, :, :].rearrange("p a t d -> p (a t) d")]
        w_hi = [att_hi[:, :, :], t_hi[:, :, :, :].rearrange("p a (t s) c -> p (a t) (s c)", s=2)]
        w_lo = [att_lo[:, :, :], t_lo[:, :, :, :].rearrange("p a (t s) c -> p (a t) (s c)", s=2)]

        ident_made = sem("ident_made")
        consts_made = sem("consts_made")
        adj_loaded = sem("adj_loaded")
        small_loaded = sem("small_loaded")
        w_loaded = sems("w_loaded", 4)
        adj_turned = sem("adj_turned")
        adj_hi_made = sem("adj_hi_made")
        adj_lo_made = sem("adj_lo_made")
        adj_off_made = sem("adj_off_made")
        exp_made = sem("exp_made")
        mix_made = sem("mix_made")
        w_hi_made = sems("w_hi_made", 4)
        w_lo_made = sems("w_lo_made", 4)
        wo_turned = sem("wo_turned")
        tri_ready = sems("tri_ready", 2)
        tri_hi_made = sems("tri_hi_made", 2)
        tri_split = sems("tri_split", 2)
        wvo_ready = sem("wvo_ready")
        wvo_hi_made = sem("wvo_hi_made")
        wvo_split = sem("wvo_split")

        dve_passed = sem("dve_passed")
        pool_passed = sem("pool_passed")
        x_loaded = sems("x_loaded", 2)
        stored = sems("stored", 2)
        stats1_made = sem("stats1_made")
        mv1_made = sem("mv1_made")
        var1_made = sem("var1_made")
        rstd1_made = sem("rstd1_made")
        y1_made = sem("y1_made")
        h1_hi_made = sem("h1_hi_made")
        h1_split = sem("h1_split")
        ah_ready = sems("ah_ready", 2)
        ah_hi_made = sems("ah_hi_made", 2)
        ah_split = sems("ah_split", 2)
        qk_copied = sem("qk_copied")
        q_part_made = sem("q_part_made")
        q_max_made = sem("q_max_made")
        qk_off_made = sem("qk_off_made")
        r_made = sem("r_made")
        r_diag_made = sem("r_diag_made")
        r_rows_ready = sem("r_rows_ready")
        r_rows_copied = sem("r_rows_copied")
        att_made = sems("att_made", 2)
        att_hi_made = sems("att_hi_made", 2)
        att_split = sems("att_split", 2)
        pair_summed = sem("pair_summed")
        three_summed = sem("three_summed")
        att_summed = sem("att_summed")
        sum_ready = sem("sum_ready")
        inv_sum_made = sem("inv_sum_made")
        msg_ready = sems("msg_ready", 2)
        msg_scaled = sems("msg_scaled", 2)
        msg_made = sems("msg_made", 2)
        x2_made = sems("x2_made", 2)
        stats2_made = sem("stats2_made")
        mv2_made = sem("mv2_made")
        var2_made = sem("var2_made")
        rstd2_made = sem("rstd2_made")
        y2_made = sem("y2_made")
        ht_ready = sems("ht_ready", 2)
        ht_hi_made = sems("ht_hi_made", 2)
        ht_split = sems("ht_split", 2)
        t_ready = [sems(f"t_ready_{k}", 2) for k in range(2)]
        t_hi_made = [sems(f"t_hi_made_{k}", 2) for k in range(2)]
        t_split = [sems(f"t_split_{k}", 2) for k in range(2)]
        y_ready = sems("y_ready", 2)
        ys_copied = sems("ys_copied", 2)
        yt_ready = sems("yt_ready", 2)
        gram_made = sems("gram_made", 2)
        diag_made = sem("diag_made")
        sq_made = sem("sq_made")
        len_clamped = sem("len_clamped")
        cols_made = sem("cols_made")
        row_diag_made = sem("row_diag_made")
        rows_ready = sem("rows_ready")
        relu_made = sem("relu_made")
        dist_made = sem("dist_made")
        lang_made = sem("lang_made")
        grav_exp_made = sem("grav_exp_made")
        grav_made = sem("grav_made")
        deg_scaled = sem("deg_scaled")
        deg_clamped = sem("deg_clamped")
        deg_inverted = sem("deg_inverted")
        deg_mixed = sem("deg_mixed")
        grav_scaled = sem("grav_scaled")
        k_made = sem("k_made")
        u_ready = sems("u_ready", 2)
        u_hi_made = sems("u_hi_made", 2)
        u_split = sems("u_split", 2)
        kt_ready = sem("kt_ready")
        kt_hi_made = sem("kt_hi_made")
        kt_split = sem("kt_split")
        agg_ready = sems("agg_ready", 2)
        out_made = sems("out_made", 2)

        def low_part(lo, full, hi, done):
            nc.vector.tensor_tensor(lo, full, hi.bitcast(F32), ALU.subtract).then_inc(done, 1)

        def product(dst, pairs):
            for n, ((lhs_hi, lhs_lo), (rhs_hi, rhs_lo)) in enumerate(pairs):
                nc.tensor.matmul(dst, lhs_lo, rhs_hi, start=(n == 0), stop=False)
                nc.tensor.matmul(dst, lhs_hi, rhs_lo, start=False, stop=False)
                last = nc.tensor.matmul(dst, lhs_hi, rhs_hi, start=False, stop=(n == len(pairs) - 1))
            return last

        def turns(eng, turn):
            turn(-2, 1)
            turn(0, 0)
            turn(0, 1)
            with eng.Fori(2, B - 3, 2) as i:
                turn(i, 0)
                turn(i, 1)
            turn(B - 2, 0)
            turn(B - 2, 1)

        def which(i, half):
            known = isinstance(i, int)
            return (not known or i + half >= 0, not known or i + half + 1 < B, not known or i + half + 2 < B)

        def dma_count(i, half, ahead):
            return i * 8 + 16 * ((half + ahead) // 2 + 1)

        block = ctx.enter_context(nc.Block())

        @block.sync
        def _(sp):
            sp.dma_start(xs[:, 0], x_v[0]).then_inc(x_loaded[0], 16)
            sp.dma_start(adj_rows[:], adj.rearrange("(t p) c -> p t c", p=P)).then_inc(adj_loaded, 16)
            sp.dma_start(w_slot[0], w_lang.rearrange("(t p) d -> p t d", p=P)).then_inc(w_loaded[0], 16)
            sp.dma_start(w_slot[1], w_grav.rearrange("(t p) d -> p t d", p=P)).then_inc(w_loaded[1], 16)
            sp.wait_ge(w_lo_made[0], 1)
            sp.dma_start(w_slot[0], w_v.rearrange("(t p) d -> p t d", p=P)).then_inc(w_loaded[2], 16)
            sp.wait_ge(w_lo_made[1], 1)
            sp.dma_start(w_slot[1], w_o.rearrange("(t p) d -> p t d", p=P)).then_inc(w_loaded[3], 16)
            sp.dma_start(xs[:, 1], x_v[1]).then_inc(x_loaded[1], 16)

            def turn(i, half):
                has_b, _, has_n = which(i, half)
                if not has_b:
                    return
                par = half
                if has_n:
                    reached(sp, x2_made[1], i + (half + 1))
                    sp.dma_start(xs[:, par], x_v[i + (half + 2)]).then_inc(x_loaded[par], 16)
                for ct in range(CT):
                    sp.wait_ge(out_made[ct], i + (half + 1))
                sp.dma_start(out_v[i + half], x2[:, par]).then_inc(stored[par], 16)

            turns(sp, turn)
            for par in range(2):
                sp.wait_ge(stored[par], 16 * (B // 2))

        @block.gpsimd
        def _(pool):
            nc.gpsimd.memset(ident[:], 0.0).then_inc(ident_made, 1)
            nc.gpsimd.memset(ones[:], 1.0).then_inc(consts_made, 1)
            nc.gpsimd.memset(minus_half[:], -0.5).then_inc(consts_made, 1)
            pool.wait_ge(ident_made, 1)
            nc.gpsimd.affine_select(out=ident[:], in_=ident[:], compare_op=ALU.not_equal, fill=1.0, base=0,
                                    pattern=[[-1, P]], channel_multiplier=1).then_inc(ident_made, 1)
            pool.wait_ge(consts_made, 2)
            pool.wait_ge(adj_loaded, 16)
            for t in range(CT):
                nc.gpsimd.affine_select(out=adj_off[:, t, :], in_=adj_rows[:, t, :], compare_op=ALU.not_equal,
                                        fill=0.0, base=P * t, pattern=[[-1, C]],
                                        channel_multiplier=1).then_inc(adj_off_made, 1)

            def norm(mv, var, rstd, made, var_made, rstd_made, count):
                reached_apart(pool, made, count, pool_passed)
                nc.gpsimd.tensor_scalar(var[:], mv[:, :, 1], LN_EPS, 1.0, ALU.add, ALU.mult).then_inc(var_made, 1)
                pool.wait_ge(var_made, count)
                nc.gpsimd.tensor_tensor(rstd[:], var[:], minus_half[:, 0:CT], ALU.pow).then_inc(rstd_made, 1)

            norm(mv1, var1, rstd1, mv1_made, var1_made, rstd1_made, 1)

            def turn(i, half):
                has_b, has_a, has_n = which(i, half)
                b_count, a_count, n_count = i + (half + 1), i + (half + 2), i + (half + 3)
                if has_a:
                    reached_apart(pool, q_part_made, a_count, pool_passed)
                    nc.gpsimd.partition_all_reduce(q_max[:], q_part[:], P, RMAX).then_inc(q_max_made, 1)
                    pool.wait_ge(r_made, a_count)
                    nc.gpsimd.tensor_tensor(r_diag[:], ident[:, None, :].to_broadcast([P, DT, P]),
                                            att_r[:, :, None].to_broadcast([P, DT, P]),
                                            ALU.mult).then_inc(r_diag_made, 1)
                if has_n:
                    norm(mv1, var1, rstd1, mv1_made, var1_made, rstd1_made, n_count)
                if has_a:
                    pool.wait_ge(att_made[0], a_count)
                    nc.gpsimd.tensor_tensor(att_sum[:], att[:, 0, :], att[:, 1, :], ALU.add).then_inc(pair_summed, 1)
                    pool.wait_ge(att_made[1], a_count)
                    pool.wait_ge(pair_summed, a_count)
                    nc.gpsimd.tensor_tensor(att_sum[:], att_sum[:], att[:, 2, :], ALU.add).then_inc(three_summed, 1)
                    pool.wait_ge(three_summed, a_count)
                    nc.gpsimd.tensor_tensor(att_sum[:], att_sum[:], att[:, 3, :], ALU.add).then_inc(att_summed, 1)
                if has_b:
                    reached_apart(pool, sq_made, b_count, pool_passed)
                    nc.gpsimd.tensor_scalar(cols[:, 0:2], sq[:, 0:2], EPS * EPS, 0.0, ALU.max,
                                            ALU.add).then_inc(len_clamped, 1)
                    nc.gpsimd.tensor_copy(cols[:, 2:4], sq[:, 2:4]).then_inc(cols_made, 1)
                    pool.wait_ge(len_clamped, b_count)
                    nc.gpsimd.tensor_tensor(cols[:, 0:2], cols[:, 0:2], minus_half[:, 0:2],
                                            ALU.pow).then_inc(cols_made, 1)
                    pool.wait_ge(cols_made, b_count * 2)
                    nc.gpsimd.tensor_tensor(diag[:], ident[:, None, :].to_broadcast([P, 4, P]),
                                            cols[:, :, None].to_broadcast([P, 4, P]),
                                            ALU.mult).then_inc(row_diag_made, 1)
                if has_a:
                    par = (half + 1) % 2
                    for ct in range(CT):
                        pool.wait_ge(msg_made[ct], a_count)
                        if ct == 0:
                            reached(pool, stored[par], dma_count(i, half, -1))
                        nc.gpsimd.tensor_tensor(x2[:, par, ct, :], xs[:, par, ct, :], msg[:, ct, :],
                                                ALU.add).then_inc(x2_made[ct], 1)
                    norm(mv2, var2, rstd2, mv2_made, var2_made, rstd2_made, a_count)

            turns(pool, turn)

        @block.scalar
        def _(act):
            act.dma_start(wqk[:, :, 0], wq.rearrange("(t p) -> p t", p=P),
                          allow_slow_non_contiguous=True).then_inc(small_loaded, 16)
            act.dma_start(wqk[:, :, 1], wk.rearrange("(t p) -> p t", p=P),
                          allow_slow_non_contiguous=True).then_inc(small_loaded, 16)
            act.dma_start(bm_col[:], bm.rearrange("(t p) -> p t", p=P),
                          allow_slow_non_contiguous=True).then_inc(small_loaded, 16)
            act.dma_start(gate[:], gate_logit.partition_broadcast(P)).then_inc(small_loaded, 16)
            act.dma_start(sigma[:], log_sigma.partition_broadcast(P)).then_inc(small_loaded, 16)
            act.wait_ge(small_loaded, 80)
            nc.scalar.activation(gate[:], gate[:], ACT.Exp, scale=-1.0).then_inc(exp_made, 1)
            nc.scalar.activation(sigma[:], sigma[:], ACT.Exp).then_inc(exp_made, 1)

            def norm_relu(count):
                act.wait_ge(y1_made, count)
                nc.scalar.activation(h1_hi[:], y1[:], ACT.Relu).then_inc(h1_hi_made, 1)

            norm_relu(1)
            nc.scalar.activation(adj_t_hi[:, :, C:C + 2], wqk[:], ACT.Copy).then_inc(adj_hi_made, 1)
            act.wait_ge(adj_turned, 1)
            nc.scalar.activation(adj_t_hi[:, :, 0:C], bank[:, 7, :].rearrange("p (t c) -> p t c", t=CT),
                                 ACT.Copy).then_inc(adj_hi_made, 1)
            for k in range(2):
                act.wait_ge(w_loaded[k], 16)
                nc.scalar.activation(w_hi[k], w_slot[k], ACT.Copy).then_inc(w_hi_made[k], 1)

            def tri(k):
                act.wait_ge(tri_ready[k], 1)
                for d in range(DT):
                    src = bank[:, 4 * k + d, :]
                    if d:
                        nc.scalar.activation(tri_hi[:, k, d, 0:d * P], src[:, 0:d * P], ACT.Copy)
                    last = nc.scalar.activation(tri_hi[:, k, d, d * P:(d + 1) * P], src[:, d * P:(d + 1) * P],
                                                ACT.Copy, scale=0.5)
                last.then_inc(tri_hi_made[k], 1)

            tri(0)
            act.wait_ge(w_loaded[2], 16)
            nc.scalar.activation(w_hi[0], w_slot[0], ACT.Copy).then_inc(w_hi_made[2], 1)
            tri(1)
            act.wait_ge(wo_turned, 1)
            nc.scalar.activation(w_hi[1], bank[:, 0:4, :], ACT.Copy).then_inc(w_hi_made[3], 1)
            act.wait_ge(wvo_ready, 1)
            nc.scalar.activation(wvo_hi[:], bank[:, 4:8, :], ACT.Copy).then_inc(wvo_hi_made, 1)

            def turn(i, half):
                has_b, has_a, has_n = which(i, half)
                b_count, a_count, n_count = i + (half + 1), i + (half + 2), i + (half + 3)
                if has_a:
                    for h in range(2):
                        act.wait_ge(ah_ready[h], a_count)
                        nc.scalar.activation(ah_hi[:, 2 * h:2 * h + 2, :], bank[:, 2 * h:2 * h + 2, 0:C],
                                             ACT.Copy).then_inc(ah_hi_made[h], 1)
                    act.wait_ge(qk_off_made, a_count)
                    nc.scalar.activation(att_r[:], k_pos[:], ACT.Exp, scale=SLOPE - 1.0).then_inc(r_made, 1)
                    nc.scalar.activation(att_a[:], q_off[:], ACT.Exp)
                    nc.scalar.activation(att_c[:], q_off[:], ACT.Exp, scale=SLOPE)
                if has_b:
                    for k in range(2):
                        for h in range(2):
                            act.wait_ge(t_ready[k][h], b_count)
                            nc.scalar.activation(
                                t_hi[:, k, 2 * h:2 * h + 2, :],
                                bank[:, 4 + 2 * k + h, :].rearrange("p (t c) -> p t c", t=2),
                                ACT.Copy).then_inc(t_hi_made[k][h], 1)
                if has_a:
                    act.wait_ge(r_rows_ready, a_count)
                    nc.scalar.activation(r_rows[:], bank[:, 0, :], ACT.Copy).then_inc(r_rows_copied, 1)
                    for h in range(2):
                        act.wait_ge(att_made[h], a_count)
                        nc.scalar.activation(att_hi[:, 2 * h:2 * h + 2, :], att[:, 2 * h:2 * h + 2, :],
                                             ACT.Copy).then_inc(att_hi_made[h], 1)
                if has_b:
                    for k in range(2):
                        act.wait_ge(y_ready[k], b_count)
                        nc.scalar.activation(ys[:, k], bank[:, 1 + k, :].rearrange("p (t c) -> p t c", t=CT),
                                             ACT.Copy).then_inc(ys_copied[k], 1)
                if has_n:
                    norm_relu(n_count)
                if has_a:
                    for ct in range(CT):
                        act.wait_ge(msg_scaled[ct], a_count)
                        nc.scalar.activation(msg[:, ct, :], msg[:, ct, :], ACT.Relu,
                                             bias=bm_col[:, ct:ct + 1]).then_inc(msg_made[ct], 1)
                if has_b:
                    act.wait_ge(dist_made, b_count)
                    for ct in range(CT):
                        last = nc.scalar.activation(grav[:, ct, :], grav[:, ct, :], ACT.Exp,
                                                    scale=neg_rate[:, 0:1], bias=g_bias[:, ct:ct + 1])
                    last.then_inc(grav_exp_made, 1)
                    for ct in range(CT):
                        act.wait_ge(u_ready[ct], b_count)
                        nc.scalar.activation(u_hi[:, ct, :], bank[:, 1 + ct, :], ACT.Copy).then_inc(u_hi_made[ct], 1)
                    act.wait_ge(kt_ready, b_count)
                    nc.scalar.activation(kt_hi[:], bank[:, 3, :].rearrange("p (t c) -> p t c", t=CT),
                                         ACT.Copy).then_inc(kt_hi_made, 1)
                if has_a:
                    for h in range(2):
                        act.wait_ge(ht_ready[h], a_count)
                        nc.scalar.activation(ht_hi[:, 2 * h:2 * h + 2, :],
                                             bank[:, 4 + 3 * h, :].rearrange("p (t c) -> p t c", t=2),
                                             ACT.Relu).then_inc(ht_hi_made[h], 1)

            turns(act, turn)

        @block.vector
        def _(dve):
            def statistics(src, stats, mv, stats_made, mv_made, ready, count):
                for ct in range(CT):
                    ready(ct)
                    last = nc.vector.bn_stats(stats[:, ct, :], src[:, ct, :])
                last.then_inc(stats_made, 1)
                reached_apart(dve, stats_made, count, dve_passed)
                for ct in range(CT):
                    last = nc.vector.bn_aggr(mv[:, ct, :], stats[:, ct, :])
                last.then_inc(mv_made, 1)

            def normed(dst, src, mv, rstd, rstd_made, made, count):
                dve.wait_ge(rstd_made, count)
                for ct in range(CT):
                    last = nc.vector.tensor_scalar(dst[:, ct, :], src[:, ct, :], mv[:, ct, 0:1], rstd[:, ct:ct + 1],
                                                   ALU.subtract, ALU.mult)
                last.then_inc(made, 1)

            def norm_stats(par, loads, count):
                def ready(ct):
                    if ct == 0:
                        dve.wait_ge(x_loaded[par], loads)
                statistics(xs[:, par], stats1, mv1, stats1_made, mv1_made, ready, count)

            def norm_apply(par, count):
                normed(y1, xs[:, par], mv1, rstd1, rstd1_made, y1_made, count)

            def norm_low(count):
                dve.wait_ge(h1_hi_made, count)
                nc.vector.scalar_tensor_tensor(out=h1_lo[:], in0=y1[:], scalar=0.0, in1=h1_hi[:].bitcast(F32),
                                               op0=ALU.max, op1=ALU.subtract).then_inc(h1_split, 1)

            norm_stats(0, 16, 1)
            norm_apply(0, 1)
            norm_low(1)
            dve.wait_ge(exp_made, 2)
            nc.vector.tensor_scalar(gate[:], gate[:], 1.0, None, ALU.add).then_inc(mix_made, 1)
            nc.vector.tensor_scalar(sigma[:], sigma[:], sigma[:, 0:1], -2.0, ALU.mult, ALU.mult).then_inc(mix_made, 1)
            dve.wait_ge(mix_made, 2)
            nc.vector.reciprocal(mix[:, 0:1], gate[:]).then_inc(mix_made, 1)
            nc.vector.reciprocal(neg_rate[:], sigma[:]).then_inc(mix_made, 1)
            dve.wait_ge(mix_made, 4)
            nc.vector.tensor_copy(mix[:, 1:2], mix[:, 0:1])
            nc.vector.tensor_scalar(mix[:, 2:3], mix[:, 0:1], -1.0, 1.0, ALU.mult, ALU.add)
            nc.vector.tensor_scalar(mix[:, 3:4], mix[:, 0:1], -1.0, 1.0, ALU.mult, ALU.add).then_inc(mix_made, 1)
            dve.wait_ge(mix_made, 5)
            nc.vector.tensor_copy(coef[:, 2:4], mix[:, 2:4])
            dve.wait_ge(adj_hi_made, 2)
            low_part(adj_t_lo[:, :, C:C + 2], wqk[:], adj_t_hi[:, :, C:C + 2], adj_lo_made)
            low_part(adj_t_lo[:, :, 0:C], bank[:, 7, :].rearrange("p (t c) -> p t c", t=CT),
                     adj_t_hi[:, :, 0:C], adj_lo_made)
            for k in range(2):
                dve.wait_ge(w_hi_made[k], 1)
                low_part(w_lo[k], w_slot[k], w_hi[k], w_lo_made[k])

            def tri(k):
                dve.wait_ge(tri_hi_made[k], 1)
                for d in range(DT):
                    src = bank[:, 4 * k + d, :]
                    if d:
                        nc.vector.tensor_tensor(tri_lo[:, k, d, 0:d * P], src[:, 0:d * P],
                                                tri_hi[:, k, d, 0:d * P].bitcast(F32), ALU.subtract)
                    own = slice(d * P, (d + 1) * P)
                    last = nc.vector.scalar_tensor_tensor(out=tri_lo[:, k, d, own], in0=src[:, own], scalar=0.5,
                                                          in1=tri_hi[:, k, d, own].bitcast(F32),
                                                          op0=ALU.mult, op1=ALU.subtract)
                last.then_inc(tri_split[k], 1)

            tri(0)
            dve.wait_ge(w_hi_made[2], 1)
            low_part(w_lo[0], w_slot[0], w_hi[0], w_lo_made[2])
            tri(1)
            dve.wait_ge(w_hi_made[3], 1)
            low_part(w_lo[1], bank[:, 0:4, :], w_hi[1], w_lo_made[3])
            dve.wait_ge(wvo_hi_made, 1)
            low_part(wvo_lo[:], bank[:, 4:8, :], wvo_hi[:], wvo_split)
            dve.wait_ge(adj_off_made, 2)

            def turn(i, half):
                has_b, has_a, has_n = which(i, half)
                b_count, a_count, n_count = i + (half + 1), i + (half + 2), i + (half + 3)
                b_par, a_par = half, (half + 1) % 2
                if has_a:
                    for h in range(2):
                        dve.wait_ge(ah_hi_made[h], a_count)
                        nc.vector.tensor_copy(qk[:, 2 * h:2 * h + 2, :],
                                              bank[:, 2 * h:2 * h + 2, C:C + 2]).then_inc(qk_copied, 1)
                        low_part(ah_lo[:, 2 * h:2 * h + 2, :], bank[:, 2 * h:2 * h + 2, 0:C],
                                 ah_hi[:, 2 * h:2 * h + 2, :], ah_split[h])
                    dve.wait_ge(qk_copied, a_count * 2)
                    nc.vector.reduce_max(q_part[:], qk[:, :, 0], AX_X).then_inc(q_part_made, 1)
                    dve.wait_ge(q_max_made, a_count)
                    nc.vector.tensor_scalar(q_off[:], qk[:, :, 0], q_max[:, 0:1], None, ALU.subtract)
                    nc.vector.tensor_scalar(k_pos[:], qk[:, :, 1], q_max[:, 0:1], 0.0, ALU.add,
                                            ALU.max).then_inc(qk_off_made, 1)
                if has_b:
                    for k in range(2):
                        for h in range(2):
                            dve.wait_ge(t_hi_made[k][h], b_count)
                            low_part(t_lo[:, k, 2 * h:2 * h + 2, :],
                                     bank[:, 4 + 2 * k + h, :].rearrange("p (t c) -> p t c", t=2),
                                     t_hi[:, k, 2 * h:2 * h + 2, :], t_split[k][h])
                if has_a:
                    dve.wait_ge(r_rows_copied, a_count)
                    for n in range(DT):
                        last = nc.vector.tensor_scalar(att[:, n, :], r_rows[:], att_c[:, n:n + 1], att_a[:, n:n + 1],
                                                       ALU.mult, ALU.max)
                        if n % 2:
                            last.then_inc(att_made[n // 2], 1)
                    for h in range(2):
                        dve.wait_ge(att_hi_made[h], a_count)
                        low_part(att_lo[:, 2 * h:2 * h + 2, :], att[:, 2 * h:2 * h + 2, :],
                                 att_hi[:, 2 * h:2 * h + 2, :], att_split[h])
                if has_n:
                    norm_stats(b_par, dma_count(i, half, 2), n_count)
                    norm_apply(b_par, n_count)
                if has_b:
                    for k in range(2):
                        dve.wait_ge(yt_ready[k], b_count)
                        nc.vector.tensor_tensor(gram[:, k], bank[:, 3 + k, :].rearrange("p (t c) -> p t c", t=CT),
                                                ys[:, k], ALU.add).then_inc(gram_made[k], 1)
                    dve.wait_ge(gram_made[1], b_count)
                    nc.vector.tensor_tensor(
                        diag[:].rearrange("p (k t) n -> p k t n", k=2),
                        gram[:].rearrange("p k t (s n) -> p k (t s) n", s=CT)[:, :, 0::CT + 1, :],
                        ident[:, None, None, :].to_broadcast([P, 2, CT, P]), ALU.mult).then_inc(diag_made, 1)
                    dve.wait_ge(diag_made, b_count)
                    nc.vector.tensor_reduce(sq[:], diag[:], AX_X, ALU.add).then_inc(sq_made, 1)
                if has_n:
                    norm_low(n_count)
                if has_a:
                    dve.wait_ge(sum_ready, a_count)
                    nc.vector.reciprocal(inv_sum[:], bank[:, 7, :]).then_inc(inv_sum_made, 1)
                    dve.wait_ge(inv_sum_made, a_count)
                    for ct in range(CT):
                        dve.wait_ge(msg_ready[ct], a_count)
                        nc.vector.tensor_tensor(msg[:, ct, :], bank[:, 5 + ct, :], inv_sum[:],
                                                ALU.mult).then_inc(msg_scaled[ct], 1)
                if has_b:
                    dve.wait_ge(rows_ready, b_count)
                    rows = bank[:, 0, :].rearrange("p (k c) -> p k c", k=2)
                    nc.vector.scalar_tensor_tensor(
                        out=lang[:], in0=gram[:, 0], scalar=0.0, in1=rows[:, 0:1, :].to_broadcast([P, CT, C]),
                        op0=ALU.max, op1=ALU.mult).then_inc(relu_made, 1)
                    nc.vector.tensor_scalar(g_bias[:], sq[:, 2:4], neg_rate[:, 0:1], None, ALU.mult)
                    nc.vector.scalar_tensor_tensor(
                        out=grav[:], in0=gram[:, 1], scalar=-2.0, in1=rows[:, 1:2, :].to_broadcast([P, CT, C]),
                        op0=ALU.mult, op1=ALU.add).then_inc(dist_made, 1)
                    dve.wait_ge(relu_made, b_count)
                    for ct in range(CT):
                        last = nc.vector.scalar_tensor_tensor(
                            out=lang[:, ct, :], in0=lang[:, ct, :], scalar=1.0, in1=adj_off[:, ct, :],
                            op0=ALU.mult, op1=ALU.mult, accum_out=deg[:, ct:ct + 1])
                    last.then_inc(lang_made, 1)
                if has_a:
                    statistics(x2[:, a_par], stats2, mv2, stats2_made, mv2_made,
                               lambda ct: dve.wait_ge(x2_made[ct], a_count), a_count)
                if has_b:
                    dve.wait_ge(grav_exp_made, b_count)
                    for ct in range(CT):
                        last = nc.vector.scalar_tensor_tensor(
                            out=grav[:, ct, :], in0=grav[:, ct, :], scalar=1.0, in1=adj_off[:, ct, :],
                            op0=ALU.min, op1=ALU.mult, accum_out=deg[:, 2 + ct:3 + ct])
                    last.then_inc(grav_made, 1)
                    dve.wait_ge(grav_made, b_count)
                    nc.vector.tensor_tensor(deg[:, 0:2], deg[:, 0:2], cols[:, 0:2], ALU.mult).then_inc(deg_scaled, 1)
                    dve.wait_ge(deg_scaled, b_count)
                    nc.vector.tensor_scalar(deg[:], deg[:], EPS, None, ALU.max).then_inc(deg_clamped, 1)
                    dve.wait_ge(deg_clamped, b_count)
                    nc.vector.tensor_tensor(coef[:, 0:2], mix[:, 0:2], cols[:, 0:2], ALU.mult)
                    nc.vector.reciprocal(deg[:], deg[:]).then_inc(deg_inverted, 1)
                    dve.wait_ge(deg_inverted, b_count)
                    nc.vector.tensor_tensor(deg[:], deg[:], coef[:], ALU.mult).then_inc(deg_mixed, 1)
                    dve.wait_ge(deg_mixed, b_count)
                    for ct in range(CT):
                        last = nc.vector.tensor_scalar(grav[:, ct, :], grav[:, ct, :], deg[:, 2 + ct:3 + ct], None,
                                                       ALU.mult)
                    last.then_inc(grav_scaled, 1)
                    dve.wait_ge(grav_scaled, b_count)
                    for ct in range(CT):
                        last = nc.vector.scalar_tensor_tensor(
                            out=lang[:, ct, :], in0=lang[:, ct, :], scalar=deg[:, ct:ct + 1], in1=grav[:, ct, :],
                            op0=ALU.mult, op1=ALU.add)
                    last.then_inc(k_made, 1)
                if has_a:
                    normed(y2, x2[:, a_par], mv2, rstd2, rstd2_made, y2_made, a_count)
                if has_b:
                    for ct in range(CT):
                        dve.wait_ge(u_hi_made[ct], b_count)
                        low_part(u_lo[:, ct, :], bank[:, 1 + ct, :], u_hi[:, ct, :], u_split[ct])
                    dve.wait_ge(kt_hi_made, b_count)
                    low_part(kt_lo[:], bank[:, 3, :].rearrange("p (t c) -> p t c", t=CT), kt_hi[:], kt_split)
                if has_a:
                    for h in range(2):
                        dve.wait_ge(ht_hi_made[h], a_count)
                        nc.vector.scalar_tensor_tensor(
                            out=ht_lo[:, 2 * h:2 * h + 2, :],
                            in0=bank[:, 4 + 3 * h, :].rearrange("p (t c) -> p t c", t=2), scalar=0.0,
                            in1=ht_hi[:, 2 * h:2 * h + 2, :].bitcast(F32),
                            op0=ALU.max, op1=ALU.subtract).then_inc(ht_split[h], 1)
                if has_b:
                    for ct in range(CT):
                        dve.wait_ge(agg_ready[ct], b_count)
                        nc.vector.tensor_tensor(x2[:, b_par, ct, :], bank[:, 5 + ct, :], x2[:, b_par, ct, :],
                                                ALU.add).then_inc(out_made[ct], 1)

            turns(dve, turn)

        @block.tensor
        def _(pe):
            def turned(dst, src, done=None):
                last = nc.tensor.transpose(dst, src, ident[:])
                if done is not None:
                    last.then_inc(done, 1)

            pe.wait_ge(ident_made, 2)
            pe.wait_ge(consts_made, 2)
            pe.wait_ge(adj_loaded, 16)
            for c in range(CT):
                for o in range(CT):
                    turned(bank[:, 7, (c * CT + o) * P:(c * CT + o + 1) * P], adj_rows[:, o, c * P:(c + 1) * P],
                           adj_turned if c == o == CT - 1 else None)
            for k in range(2):
                pe.wait_ge(w_lo_made[k], 1)
                if k == 1:
                    pe.wait_ge(adj_lo_made, 2)
                for d in range(DT):
                    last = product(bank[:, 4 * k + d, 0:TRI[d]],
                                   [((w_hi[k][:, t, d * P:(d + 1) * P], w_lo[k][:, t, d * P:(d + 1) * P]),
                                     (w_hi[k][:, t, 0:TRI[d]], w_lo[k][:, t, 0:TRI[d]])) for t in range(DT)])
                last.then_inc(tri_ready[k], 1)
            pe.wait_ge(tri_split[0], 1)
            pe.wait_ge(w_loaded[3], 16)
            for t in range(DT):
                for e in range(DT):
                    turned(bank[:, t, e * P:(e + 1) * P], w_slot[1][:, e, t * P:(t + 1) * P],
                           wo_turned if t == e == DT - 1 else None)
            pe.wait_ge(tri_split[1], 1)
            pe.wait_ge(w_lo_made[2], 1)
            pe.wait_ge(w_lo_made[3], 1)
            for d in range(DT):
                last = product(bank[:, 4 + d, :],
                               [((w_hi[0][:, t, d * P:(d + 1) * P], w_lo[0][:, t, d * P:(d + 1) * P]),
                                 (w_hi[1][:, t, :], w_lo[1][:, t, :])) for t in range(DT)])
            last.then_inc(wvo_ready, 1)
            pe.wait_ge(wvo_split, 1)

            def turn(i, half):
                has_b, has_a, _ = which(i, half)
                b_count, a_count = i + (half + 1), i + (half + 2)
                if has_a:
                    pe.wait_ge(h1_split, a_count)
                    reached(pe, kt_split, i + half)
                    for n in range(DT):
                        nodes = slice(n * P, (n + 1) * P)
                        last = product(bank[:, n, 0:C + 2],
                                       [((h1_hi[:, c, nodes], h1_lo[:, c, nodes]),
                                         (adj_t_hi[:, c, :], adj_t_lo[:, c, :])) for c in range(CT)])
                        if n % 2:
                            last.then_inc(ah_ready[n // 2], 1)
                if has_b:
                    for h in range(2):
                        pe.wait_ge(ht_split[h], b_count)
                    for k in range(2):
                        for h in range(2):
                            if 2 * k + h in (1, 2):
                                reached(pe, out_made[2 * k + h - 1], i + half)
                            for s in range(2):
                                e = 2 * h + s
                                last = product(bank[:, 4 + 2 * k + h, s * C:(s + 1) * C],
                                               [((tri_hi[:, k, d, e * P:(e + 1) * P],
                                                  tri_lo[:, k, d, e * P:(e + 1) * P]),
                                                 (ht_hi[:, d, :], ht_lo[:, d, :])) for d in range(e, DT)])
                            last.then_inc(t_ready[k][h], 1)
                if has_a:
                    pe.wait_ge(r_diag_made, a_count)
                    pe.wait_ge(ah_split[0], a_count)
                    nc.tensor.matmul(bank[:, 0, :], ones[:], r_diag[:].rearrange("p t n -> p (t n)"),
                                     start=True, stop=True).then_inc(r_rows_ready, 1)
                    pe.wait_ge(ah_split[1], a_count)
                if has_b:
                    for k in range(2):
                        for h in range(2):
                            pe.wait_ge(t_split[k][h], b_count)
                        for t in range(CT):
                            nodes = slice(t * P, (t + 1) * P)
                            last = product(bank[:, 1 + k, t * C:(t + 1) * C],
                                           [((t_hi[:, k, e, nodes], t_lo[:, k, e, nodes]),
                                             (ht_hi[:, e, :], ht_lo[:, e, :])) for e in range(DT)])
                        last.then_inc(y_ready[k], 1)
                    for k in range(2):
                        pe.wait_ge(ys_copied[k], b_count)
                        for t in range(CT):
                            for s in range(CT):
                                turned(bank[:, 3 + k, (t * CT + s) * P:(t * CT + s + 1) * P],
                                       ys[:, k, s, t * P:(t + 1) * P], yt_ready[k] if t == s == CT - 1 else None)

                def messages(ct):
                    outs = slice(ct * P, (ct + 1) * P)
                    product(bank[:, 5 + ct, :],
                            [((ah_hi[:, n, outs], ah_lo[:, n, outs]),
                              (att_hi[:, n, :], att_lo[:, n, :])) for n in range(DT)]).then_inc(msg_ready[ct], 1)

                if has_a:
                    for h in range(2):
                        pe.wait_ge(att_split[h], a_count)
                    messages(0)
                    pe.wait_ge(att_summed, a_count)
                    nc.tensor.matmul(bank[:, 7, :], ones[:], att_sum[:], start=True, stop=True).then_inc(sum_ready, 1)
                    messages(1)
                if has_b:
                    pe.wait_ge(row_diag_made, b_count)
                    if has_a:
                        pe.wait_ge(r_rows_copied, a_count)
                    nc.tensor.matmul(bank[:, 0, :], ones[:], diag[:].rearrange("p t n -> p (t n)"),
                                     start=True, stop=True).then_inc(rows_ready, 1)
                    for t in range(CT):
                        nodes = slice(t * P, (t + 1) * P)
                        product(bank[:, 1 + t, :],
                                [((ht_hi[:, d, nodes], ht_lo[:, d, nodes]),
                                  (wvo_hi[:, d, :], wvo_lo[:, d, :])) for d in range(DT)]).then_inc(u_ready[t], 1)
                    pe.wait_ge(k_made, b_count)
                    for t in range(CT):
                        for s in range(CT):
                            turned(bank[:, 3, (t * CT + s) * P:(t * CT + s + 1) * P],
                                   lang[:, s, t * P:(t + 1) * P], kt_ready if t == s == CT - 1 else None)
                if has_a:
                    pe.wait_ge(y2_made, a_count)
                    for h in range(2):
                        for s in range(2):
                            d = 2 * h + s
                            for t in range(CT):
                                turned(bank[:, 4 + 3 * h, (s * CT + t) * P:(s * CT + t + 1) * P],
                                       y2[:, t, d * P:(d + 1) * P], ht_ready[h] if s == t == 1 else None)
                if has_b:
                    pe.wait_ge(kt_split, b_count)
                    for t in range(CT):
                        nodes = slice(t * P, (t + 1) * P)
                        product(bank[:, 5 + t, :],
                                [((kt_hi[:, m, nodes], kt_lo[:, m, nodes]),
                                  (u_hi[:, m, :], u_lo[:, m, :])) for m in range(CT)]).then_inc(agg_ready[t], 1)

            turns(pe, turn)


_INS = ["x", "adj", "L0_gnn_wq", "L0_gnn_wk", "L0_gnn_bm", "L1_gnn_W_lang", "L1_gnn_W_grav", "L1_gnn_W_V",
        "L1_gnn_W_O", "L1_gnn_gate_logit", "L1_gnn_log_sigma"]


def kernel(**inputs):
    import numpy as _np
    import concourse.bacc as _bacc
    from concourse import mybir as _mybir
    from concourse.bass_utils import run_bass_kernel_spmd as _run

    nc = _bacc.Bacc("TRN2", target_bir_lowering=False, num_devices=1)
    arrays, args = {}, []
    for name in _INS:
        a = _np.ascontiguousarray(inputs[name])
        if a.ndim == 0:
            a = a.reshape(1)
        arrays[f"in_{name}"] = a
        args.append(nc.dram_tensor(f"in_{name}", a.shape, _mybir.dt.from_np(a.dtype), kind="ExternalInput").ap())
    shape = inputs["x"].shape
    args.append(nc.dram_tensor("out_x", shape, _mybir.dt.float32, kind="ExternalOutput").ap())
    program(nc, *args)
    r = _run(nc, [arrays], core_ids=[0])
    return r.results[0]["out_x"]
```

```python
from contextlib import ExitStack

import concourse.bass as bass
from concourse import mybir

P = 128
F32 = mybir.dt.float32
F32R = mybir.dt.float32r
ALU = mybir.AluOpType
ACT = mybir.ActivationFunctionType
AX_X = mybir.AxisListType.X
RMAX = bass.bass_isa.ReduceOp.max

SLOPE = 0.01
LN_EPS = 1e-5
EPS = 1e-8


def reached(eng, semaphore, count):
    if not (isinstance(count, int) and count <= 0):
        eng.wait_ge(semaphore, count)


def reached_apart(eng, semaphore, count, passed):
    eng.wait_ge(semaphore, count)
    if not isinstance(count, int):
        eng.sem_inc(passed, 1)


def program(nc, x, adj, wq, wk, bm, w_lang, w_grav, w_v, w_o, gate_logit, log_sigma, out):
    B, C, D = x.shape
    CT = C // P
    DT = D // P
    TRI = [max((d + 1) * P, 2 * P) for d in range(DT)]
    assert C == 2 * P and D == 4 * P and B % 2 == 0 and B >= 4

    x_v = x.rearrange("b (t p) d -> b p t d", p=P)
    out_v = out.rearrange("b (t p) d -> b p t d", p=P)

    with ExitStack() as ctx:
        def sb(name, shape, dt=F32):
            return ctx.enter_context(nc.sbuf_tensor(name, shape, dt))

        def sem(name):
            return ctx.enter_context(nc.semaphore(name))

        def sems(name, n):
            return [sem(f"{name}_{k}") for k in range(n)]

        ident = sb("ident", [P, P])
        ones = sb("ones", [P, P], F32R)
        minus_half = sb("minus_half", [P, 4])
        adj_rows = sb("adj_rows", [P, CT, C])
        adj_off = sb("adj_off", [P, CT, C])
        wqk = sb("wqk", [P, CT, 2])
        adj_t_hi = sb("adj_t_hi", [P, CT, C + 2], F32R)
        adj_t_lo = sb("adj_t_lo", [P, CT, C + 2], F32R)
        bm_col = sb("bm_col", [P, CT])
        gate = sb("gate", [P, 1])
        sigma = sb("sigma", [P, 1])
        mix = sb("mix", [P, 4])
        neg_rate = sb("neg_rate", [P, 1])
        tri_hi = sb("tri_hi", [P, 2, DT, D], F32R)
        tri_lo = sb("tri_lo", [P, 2, DT, D], F32R)
        wvo_hi = sb("wvo_hi", [P, DT, D], F32R)
        wvo_lo = sb("wvo_lo", [P, DT, D], F32R)

        xs = sb("xs", [P, 2, CT, D])
        x2 = sb("x2", [P, 2, CT, D])
        stats1 = sb("stats1", [P, CT, 6])
        mv1 = sb("mv1", [P, CT, 2])
        var1 = sb("var1", [P, CT])
        rstd1 = sb("rstd1", [P, CT])
        shift1 = sb("shift1", [P, CT])
        normed = sb("normed", [P, CT, D])
        h1_hi = sb("h1_hi", [P, CT, D], F32R)
        h1_lo = sb("h1_lo", [P, CT, D], F32R)
        ah_hi = sb("ah_hi", [P, DT, C], F32R)
        ah_lo = sb("ah_lo", [P, DT, C], F32R)
        qk = sb("qk", [P, DT, 2])
        q_part = sb("q_part", [P, 1])
        q_max = sb("q_max", [P, 1])
        q_off = sb("q_off", [P, DT])
        k_pos = sb("k_pos", [P, DT])
        att_a = sb("att_a", [P, DT])
        att_c = sb("att_c", [P, DT])
        att_r = sb("att_r", [P, DT])
        r_hi = sb("r_hi", [P, DT], F32R)
        r_parts = sb("r_parts", [P, 2 * DT])
        r_diag = sb("r_diag", [P, 2 * DT, P], F32R)
        r_rows = sb("r_rows", [P, D])
        att = sb("att", [P, DT, D])
        att_hi = sb("att_hi", [P, DT, D], F32R)
        att_lo = sb("att_lo", [P, DT, D], F32R)
        att_sum = sb("att_sum", [P, D])
        sum_hi = sb("sum_hi", [P, D], F32R)
        sum_lo = sb("sum_lo", [P, D], F32R)
        inv_sum = sb("inv_sum", [P, D])
        msg = sb("msg", [P, CT, D])
        stats2 = sb("stats2", [P, CT, 6])
        mv2 = sb("mv2", [P, CT, 2])
        var2 = sb("var2", [P, CT])
        rstd2 = sb("rstd2", [P, CT])
        shift2 = sb("shift2", [P, CT])
        ht_hi = sb("ht_hi", [P, DT, C], F32R)
        ht_lo = sb("ht_lo", [P, DT, C], F32R)
        t_hi = sb("t_hi", [P, 2, DT, C], F32R)
        t_lo = sb("t_lo", [P, 2, DT, C], F32R)
        ys = sb("ys", [P, 2, CT, C])
        gram = sb("gram", [P, 2, CT, C])
        diag = sb("diag", [P, 8, P], F32R)
        own = sb("own", [P, 4, P])
        sq = sb("sq", [P, 4])
        cols = sb("cols", [P, 4])
        cols_hi = sb("cols_hi", [P, 4], F32R)
        col_parts = sb("col_parts", [P, 8])
        coef = sb("coef", [P, 4])
        g_bias = sb("g_bias", [P, CT])
        deg = sb("deg", [P, 4])
        lang = sb("lang", [P, CT, C])
        grav = sb("grav", [P, CT, C])
        u_hi = sb("u_hi", [P, CT, D], F32R)
        u_lo = sb("u_lo", [P, CT, D], F32R)
        kt_hi = sb("kt_hi", [P, CT, C], F32R)
        kt_lo = sb("kt_lo", [P, CT, C], F32R)

        bank = ctx.enter_context(nc.psum_tensor("bank", [P, 8, 512], F32))

        w_slot = [att[:, :, :], x2[:, :, :, :].rearrange("p a t d -> p (a t) d")]
        w_hi = [att_hi[:, :, :], t_hi[:, :, :, :].rearrange("p a (t s) c -> p (a t) (s c)", s=2)]
        w_lo = [att_lo[:, :, :], t_lo[:, :, :, :].rearrange("p a (t s) c -> p (a t) (s c)", s=2)]

        ident_made = sem("ident_made")
        consts_made = sem("consts_made")
        adj_loaded = sem("adj_loaded")
        small_loaded = sem("small_loaded")
        w_loaded = sems("w_loaded", 4)
        adj_turned = sem("adj_turned")
        adj_hi_made = sem("adj_hi_made")
        adj_lo_made = sem("adj_lo_made")
        adj_off_made = sem("adj_off_made")
        exp_made = sem("exp_made")
        mix_made = sem("mix_made")
        w_hi_made = sems("w_hi_made", 4)
        w_lo_made = sems("w_lo_made", 4)
        wo_turned = sem("wo_turned")
        tri_ready = sems("tri_ready", 2)
        tri_hi_made = sems("tri_hi_made", 2)
        tri_split = sems("tri_split", 2)
        wvo_ready = sem("wvo_ready")
        wvo_hi_made = sem("wvo_hi_made")
        wvo_split = sem("wvo_split")

        dve_passed = sem("dve_passed")
        pool_passed = sem("pool_passed")
        x_loaded = sems("x_loaded", 2)
        stored = sems("stored", 2)
        stats1_made = sem("stats1_made")
        mv1_made = sem("mv1_made")
        var1_made = sem("var1_made")
        rstd1_made = sem("rstd1_made")
        shift1_made = sem("shift1_made")
        normed1_made = sem("normed1_made")
        h1_hi_made = sem("h1_hi_made")
        h1_split = sem("h1_split")
        ah_ready = sems("ah_ready", 2)
        ah_hi_made = sems("ah_hi_made", 2)
        ah_split = sems("ah_split", 2)
        qk_copied = sem("qk_copied")
        q_part_made = sem("q_part_made")
        q_max_made = sem("q_max_made")
        qk_off_made = sem("qk_off_made")
        r_made = sem("r_made")
        r_split = sem("r_split")
        r_diag_made = sem("r_diag_made")
        r_rows_ready = sem("r_rows_ready")
        r_rows_copied = sem("r_rows_copied")
        att_made = sems("att_made", 2)
        att_hi_made = sems("att_hi_made", 2)
        att_split = sems("att_split", 2)
        att_tail_split = sem("att_tail_split")
        pair_summed = sem("pair_summed")
        three_summed = sem("three_summed")
        att_summed = sem("att_summed")
        sum_hi_made = sem("sum_hi_made")
        sum_split = sem("sum_split")
        sum_ready = sem("sum_ready")
        inv_sum_made = sem("inv_sum_made")
        msg_ready = sems("msg_ready", 2)
        msg_scaled = sems("msg_scaled", 2)
        msg_made = sems("msg_made", 2)
        x2_made = sems("x2_made", 2)
        stats2_made = sem("stats2_made")
        mv2_made = sem("mv2_made")
        var2_made = sem("var2_made")
        rstd2_made = sem("rstd2_made")
        shift2_made = sem("shift2_made")
        normed_made = sem("normed_made")
        ht_ready = sems("ht_ready", 2)
        ht_hi_made = sems("ht_hi_made", 2)
        ht_split = sems("ht_split", 2)
        t_ready = [sems(f"t_ready_{k}", 2) for k in range(2)]
        t_hi_made = [sems(f"t_hi_made_{k}", 2) for k in range(2)]
        t_split = [sems(f"t_split_{k}", 2) for k in range(2)]
        y_ready = sems("y_ready", 2)
        ys_copied = sems("ys_copied", 2)
        yt_ready = sems("yt_ready", 2)
        gram_made = sems("gram_made", 2)
        sq_made = sem("sq_made")
        len_clamped = sem("len_clamped")
        cols_made = sem("cols_made")
        cols_hi_made = sem("cols_hi_made")
        cols_split = sem("cols_split")
        row_diag_made = sem("row_diag_made")
        rows_ready = sem("rows_ready")
        relu_made = sem("relu_made")
        dist_made = sem("dist_made")
        lang_made = sem("lang_made")
        grav_exp_made = sem("grav_exp_made")
        grav_made = sem("grav_made")
        deg_scaled = sem("deg_scaled")
        deg_clamped = sem("deg_clamped")
        deg_inverted = sem("deg_inverted")
        deg_mixed = sem("deg_mixed")
        grav_scaled = sem("grav_scaled")
        k_made = sem("k_made")
        u_ready = sems("u_ready", 2)
        u_hi_made = sems("u_hi_made", 2)
        u_split = sems("u_split", 2)
        kt_ready = sem("kt_ready")
        kt_hi_made = sem("kt_hi_made")
        kt_split = sem("kt_split")
        agg_ready = sems("agg_ready", 2)
        out_made = sems("out_made", 2)

        def low_part(lo, full, hi, done):
            nc.vector.tensor_tensor(lo, full, hi.bitcast(F32), ALU.subtract).then_inc(done, 1)

        def product(dst, pairs):
            for n, ((lhs_hi, lhs_lo), (rhs_hi, rhs_lo)) in enumerate(pairs):
                nc.tensor.matmul(dst, lhs_lo, rhs_hi, start=(n == 0), stop=False)
                nc.tensor.matmul(dst, lhs_hi, rhs_lo, start=False, stop=False)
                last = nc.tensor.matmul(dst, lhs_hi, rhs_hi, start=False, stop=(n == len(pairs) - 1))
            return last

        def turns(eng, turn):
            turn(-2, 1)
            turn(0, 0)
            turn(0, 1)
            with eng.Fori(2, B - 3, 2) as i:
                turn(i, 0)
                turn(i, 1)
            turn(B - 2, 0)
            turn(B - 2, 1)
            turn(B, 0)

        def which(i, half):
            if not isinstance(i, int):
                return True, True, True, True
            return tuple(0 <= i + half + ahead < B for ahead in (-1, 0, 1, 2))

        def dma_count(i, half, ahead):
            return i * 8 + 16 * ((half + ahead) // 2 + 1)

        block = ctx.enter_context(nc.Block())

        @block.sync
        def _(sp):
            sp.dma_start(xs[:, 0], x_v[0]).then_inc(x_loaded[0], 16)
            sp.dma_start(adj_rows[:], adj.rearrange("(t p) c -> p t c", p=P)).then_inc(adj_loaded, 16)
            sp.dma_start(w_slot[0], w_lang.rearrange("(t p) d -> p t d", p=P)).then_inc(w_loaded[0], 16)
            sp.dma_start(w_slot[1], w_grav.rearrange("(t p) d -> p t d", p=P)).then_inc(w_loaded[1], 16)
            sp.wait_ge(w_lo_made[0], 1)
            sp.dma_start(w_slot[0], w_v.rearrange("(t p) d -> p t d", p=P)).then_inc(w_loaded[2], 16)
            sp.wait_ge(w_lo_made[1], 1)
            sp.dma_start(w_slot[1], w_o.rearrange("(t p) d -> p t d", p=P)).then_inc(w_loaded[3], 16)
            sp.dma_start(xs[:, 1], x_v[1]).then_inc(x_loaded[1], 16)

            def turn(i, half):
                has_k, has_b, _, has_n = which(i, half)
                if has_b and has_n:
                    sp.wait_ge(x2_made[1], i + (half + 1))
                    sp.dma_start(xs[:, half], x_v[i + (half + 2)]).then_inc(x_loaded[half], 16)
                if has_k:
                    for ct in range(CT):
                        sp.wait_ge(out_made[ct], i + half)
                    sp.dma_start(out_v[i + (half - 1)], x2[:, 1 - half]).then_inc(stored[1 - half], 16)

            turns(sp, turn)
            for par in range(2):
                sp.wait_ge(stored[par], 16 * (B // 2))

        @block.gpsimd
        def _(pool):
            nc.gpsimd.memset(ident[:], 0.0).then_inc(ident_made, 1)
            nc.gpsimd.memset(ones[:].bitcast(F32), 1.0).then_inc(consts_made, 1)
            nc.gpsimd.memset(minus_half[:], -0.5).then_inc(consts_made, 1)
            pool.wait_ge(ident_made, 1)
            nc.gpsimd.affine_select(out=ident[:], in_=ident[:], compare_op=ALU.not_equal, fill=1.0, base=0,
                                    pattern=[[-1, P]], channel_multiplier=1).then_inc(ident_made, 1)
            pool.wait_ge(consts_made, 2)
            pool.wait_ge(adj_loaded, 16)
            for t in range(CT):
                nc.gpsimd.affine_select(out=adj_off[:, t, :], in_=adj_rows[:, t, :], compare_op=ALU.not_equal,
                                        fill=0.0, base=P * t, pattern=[[-1, C]],
                                        channel_multiplier=1).then_inc(adj_off_made, 1)

            def norm(mv, var, rstd, shift, mv_made, var_made, rstd_made, shift_made, count):
                reached_apart(pool, mv_made, count, pool_passed)
                nc.gpsimd.tensor_scalar(var[:], mv[:, :, 1], LN_EPS, 1.0, ALU.add, ALU.mult).then_inc(var_made, 1)
                nc.gpsimd.tensor_scalar(shift[:], mv[:, :, 0], -1.0, 0.0, ALU.mult, ALU.add).then_inc(var_made, 1)
                pool.wait_ge(var_made, 2 * count)
                nc.gpsimd.tensor_tensor(rstd[:], var[:], minus_half[:, 0:CT], ALU.pow).then_inc(rstd_made, 1)
                pool.wait_ge(rstd_made, count)
                nc.gpsimd.tensor_tensor(shift[:], shift[:], rstd[:], ALU.mult).then_inc(shift_made, 1)

            norm_n = (mv1, var1, rstd1, shift1, mv1_made, var1_made, rstd1_made, shift1_made)
            norm_a = (mv2, var2, rstd2, shift2, mv2_made, var2_made, rstd2_made, shift2_made)
            norm(*norm_n, 1)

            def turn(i, half):
                _, has_b, has_a, has_n = which(i, half)
                b_count, a_count, n_count = i + (half + 1), i + (half + 2), i + (half + 3)
                if has_a:
                    reached_apart(pool, q_part_made, a_count, pool_passed)
                    nc.gpsimd.partition_all_reduce(q_max[:], q_part[:], P, RMAX).then_inc(q_max_made, 1)
                    pool.wait_ge(r_made, a_count)
                    nc.gpsimd.tensor_tensor(r_parts[:, DT:2 * DT], att_r[:], r_hi[:].bitcast(F32),
                                            ALU.subtract).then_inc(r_split, 1)
                    nc.gpsimd.tensor_copy(r_parts[:, 0:DT], r_hi[:].bitcast(F32)).then_inc(r_split, 1)
                    pool.wait_ge(r_split, 2 * a_count)
                    nc.gpsimd.tensor_tensor(r_diag[:], ident[:, None, :].to_broadcast([P, 2 * DT, P]),
                                            r_parts[:, :, None].to_broadcast([P, 2 * DT, P]),
                                            ALU.mult).then_inc(r_diag_made, 1)
                if has_n:
                    norm(*norm_n, n_count)
                if has_a:
                    pool.wait_ge(att_made[0], a_count)
                    nc.gpsimd.tensor_tensor(att_sum[:], att[:, 0, :], att[:, 1, :], ALU.add).then_inc(pair_summed, 1)
                    pool.wait_ge(att_made[1], a_count)
                    pool.wait_ge(pair_summed, a_count)
                    nc.gpsimd.tensor_tensor(att_sum[:], att_sum[:], att[:, 2, :], ALU.add).then_inc(three_summed, 1)
                    pool.wait_ge(three_summed, a_count)
                    nc.gpsimd.tensor_tensor(att_sum[:], att_sum[:], att[:, 3, :], ALU.add).then_inc(att_summed, 1)
                    pool.wait_ge(sum_hi_made, a_count)
                    nc.gpsimd.tensor_tensor(sum_lo[:], att_sum[:], sum_hi[:].bitcast(F32),
                                            ALU.subtract).then_inc(sum_split, 1)
                    pool.wait_ge(att_hi_made[1], a_count)
                    nc.gpsimd.tensor_tensor(att_lo[:, 3, :], att[:, 3, :], att_hi[:, 3, :].bitcast(F32),
                                            ALU.subtract).then_inc(att_tail_split, 1)
                if has_b:
                    reached_apart(pool, sq_made, b_count, pool_passed)
                    nc.gpsimd.tensor_scalar(cols[:, 0:2], sq[:, 0:2], EPS * EPS, 0.0, ALU.max,
                                            ALU.add).then_inc(len_clamped, 1)
                    nc.gpsimd.tensor_copy(cols[:, 2:4], sq[:, 2:4]).then_inc(cols_made, 1)
                    pool.wait_ge(len_clamped, b_count)
                    nc.gpsimd.tensor_tensor(cols[:, 0:2], cols[:, 0:2], minus_half[:, 0:2],
                                            ALU.pow).then_inc(cols_made, 1)
                    pool.wait_ge(cols_made, b_count * 2)
                    nc.gpsimd.tensor_tensor(cols_hi[:], cols[:], ones[:, 0:4].bitcast(F32),
                                            ALU.mult).then_inc(cols_hi_made, 1)
                    pool.wait_ge(cols_hi_made, b_count)
                    nc.gpsimd.tensor_tensor(col_parts[:, 4:8], cols[:], cols_hi[:].bitcast(F32),
                                            ALU.subtract).then_inc(cols_split, 1)
                    nc.gpsimd.tensor_copy(col_parts[:, 0:4], cols_hi[:].bitcast(F32)).then_inc(cols_split, 1)
                    pool.wait_ge(cols_split, 2 * b_count)
                    nc.gpsimd.tensor_tensor(diag[:], ident[:, None, :].to_broadcast([P, 8, P]),
                                            col_parts[:, :, None].to_broadcast([P, 8, P]),
                                            ALU.mult).then_inc(row_diag_made, 1)
                if has_a:
                    par = (half + 1) % 2
                    for ct in range(CT):
                        pool.wait_ge(msg_made[ct], a_count)
                        if ct == 0:
                            reached(pool, stored[par], dma_count(i, half, -1))
                        nc.gpsimd.tensor_tensor(x2[:, par, ct, :], xs[:, par, ct, :], msg[:, ct, :],
                                                ALU.add).then_inc(x2_made[ct], 1)
                    norm(*norm_a, a_count)

            turns(pool, turn)

        @block.scalar
        def _(act):
            act.dma_start(wqk[:, :, 0], wq.rearrange("(t p) -> p t", p=P),
                          allow_slow_non_contiguous=True).then_inc(small_loaded, 16)
            act.dma_start(wqk[:, :, 1], wk.rearrange("(t p) -> p t", p=P),
                          allow_slow_non_contiguous=True).then_inc(small_loaded, 16)
            act.dma_start(bm_col[:], bm.rearrange("(t p) -> p t", p=P),
                          allow_slow_non_contiguous=True).then_inc(small_loaded, 16)
            act.dma_start(gate[:], gate_logit.partition_broadcast(P)).then_inc(small_loaded, 16)
            act.dma_start(sigma[:], log_sigma.partition_broadcast(P)).then_inc(small_loaded, 16)
            act.wait_ge(small_loaded, 80)
            nc.scalar.activation(gate[:], gate[:], ACT.Exp, scale=-1.0).then_inc(exp_made, 1)
            nc.scalar.activation(sigma[:], sigma[:], ACT.Exp).then_inc(exp_made, 1)

            def norm_relu(par, count):
                act.wait_ge(shift1_made, count)
                for ct in range(CT):
                    last = nc.scalar.activation(normed[:, ct, :], xs[:, par, ct, :], ACT.Identity,
                                                scale=rstd1[:, ct:ct + 1], bias=shift1[:, ct:ct + 1])
                last.then_inc(normed1_made, 1)
                act.wait_ge(normed1_made, count)
                nc.scalar.activation(h1_hi[:], normed[:], ACT.Relu).then_inc(h1_hi_made, 1)

            norm_relu(0, 1)
            nc.scalar.activation(adj_t_hi[:, :, C:C + 2], wqk[:], ACT.Copy).then_inc(adj_hi_made, 1)
            act.wait_ge(adj_turned, 1)
            nc.scalar.activation(adj_t_hi[:, :, 0:C], bank[:, 7, :].rearrange("p (t c) -> p t c", t=CT),
                                 ACT.Copy).then_inc(adj_hi_made, 1)
            for k in range(2):
                act.wait_ge(w_loaded[k], 16)
                nc.scalar.activation(w_hi[k], w_slot[k], ACT.Copy).then_inc(w_hi_made[k], 1)

            def tri(k):
                act.wait_ge(tri_ready[k], 1)
                for d in range(DT):
                    src = bank[:, 4 * k + d, :]
                    if d:
                        nc.scalar.activation(tri_hi[:, k, d, 0:d * P], src[:, 0:d * P], ACT.Copy)
                    last = nc.scalar.activation(tri_hi[:, k, d, d * P:(d + 1) * P], src[:, d * P:(d + 1) * P],
                                                ACT.Copy, scale=0.5)
                last.then_inc(tri_hi_made[k], 1)

            tri(0)
            act.wait_ge(w_loaded[2], 16)
            nc.scalar.activation(w_hi[0], w_slot[0], ACT.Copy).then_inc(w_hi_made[2], 1)
            tri(1)
            act.wait_ge(wo_turned, 1)
            nc.scalar.activation(w_hi[1], bank[:, 0:4, :], ACT.Copy).then_inc(w_hi_made[3], 1)
            act.wait_ge(wvo_ready, 1)
            nc.scalar.activation(wvo_hi[:], bank[:, 4:8, :], ACT.Copy).then_inc(wvo_hi_made, 1)

            def turn(i, half):
                has_k, has_b, has_a, has_n = which(i, half)
                k_count, b_count, a_count, n_count = i + half, i + (half + 1), i + (half + 2), i + (half + 3)
                def features_high(h):
                    act.wait_ge(ah_ready[h], a_count)
                    nc.scalar.activation(ah_hi[:, 2 * h:2 * h + 2, :], bank[:, 2 * h:2 * h + 2, 0:C],
                                         ACT.Copy).then_inc(ah_hi_made[h], 1)

                if has_a:
                    features_high(0)
                if has_k:
                    act.wait_ge(kt_ready, k_count)
                    nc.scalar.activation(kt_hi[:], bank[:, 6, :].rearrange("p (t c) -> p t c", t=CT),
                                         ACT.Copy).then_inc(kt_hi_made, 1)
                if has_b:
                    for h in range(2):
                        act.wait_ge(ht_ready[h], b_count)
                        nc.scalar.activation(ht_hi[:, 2 * h:2 * h + 2, :],
                                             bank[:, 4 + 3 * h, :].rearrange("p (t c) -> p t c", t=2),
                                             ACT.Relu).then_inc(ht_hi_made[h], 1)
                if has_a:
                    features_high(1)
                if has_a:
                    act.wait_ge(qk_off_made, a_count)
                    nc.scalar.activation(att_r[:], k_pos[:], ACT.Exp, scale=SLOPE - 1.0)
                    nc.scalar.activation(r_hi[:], k_pos[:], ACT.Exp, scale=SLOPE - 1.0).then_inc(r_made, 1)
                    nc.scalar.activation(att_a[:], q_off[:], ACT.Exp)
                    nc.scalar.activation(att_c[:], q_off[:], ACT.Exp, scale=SLOPE)

                def t_high(k):
                    for h in range(2):
                        act.wait_ge(t_ready[k][h], b_count)
                        nc.scalar.activation(t_hi[:, k, 2 * h:2 * h + 2, :],
                                             bank[:, 4 + 2 * k + h, :].rearrange("p (t c) -> p t c", t=2),
                                             ACT.Copy).then_inc(t_hi_made[k][h], 1)

                if has_b:
                    t_high(0)
                if has_a:
                    act.wait_ge(r_rows_ready, a_count)
                    nc.scalar.activation(r_rows[:], bank[:, 2, :], ACT.Copy).then_inc(r_rows_copied, 1)
                if has_n:
                    norm_relu(half, n_count)
                if has_b:
                    t_high(1)
                if has_a:
                    for h in range(2):
                        act.wait_ge(att_made[h], a_count)
                        nc.scalar.activation(att_hi[:, 2 * h:2 * h + 2, :], att[:, 2 * h:2 * h + 2, :],
                                             ACT.Copy).then_inc(att_hi_made[h], 1)
                if has_a:
                    act.wait_ge(att_summed, a_count)
                    nc.scalar.activation(sum_hi[:], att_sum[:], ACT.Copy).then_inc(sum_hi_made, 1)
                if has_b:
                    for k in range(2):
                        act.wait_ge(y_ready[k], b_count)
                        nc.scalar.activation(ys[:, k], bank[:, 1 + k, :].rearrange("p (t c) -> p t c", t=CT),
                                             ACT.Copy).then_inc(ys_copied[k], 1)
                if has_a:
                    for ct in range(CT):
                        act.wait_ge(msg_scaled[ct], a_count)
                        nc.scalar.activation(msg[:, ct, :], msg[:, ct, :], ACT.Relu,
                                             bias=bm_col[:, ct:ct + 1]).then_inc(msg_made[ct], 1)
                if has_b:
                    act.wait_ge(dist_made, b_count)
                    for t in range(CT):
                        last = nc.scalar.activation(grav[:, t, :], grav[:, t, :], ACT.Exp,
                                                    scale=neg_rate[:, 0:1], bias=g_bias[:, t:t + 1])
                    last.then_inc(grav_exp_made, 1)
                    for ct in range(CT):
                        act.wait_ge(u_ready[ct], b_count)
                        nc.scalar.activation(u_hi[:, ct, :], bank[:, 1 + ct, :], ACT.Copy).then_inc(u_hi_made[ct], 1)
                if has_a:
                    act.wait_ge(shift2_made, a_count)
                    for ct in range(CT):
                        last = nc.scalar.activation(normed[:, ct, :], x2[:, (half + 1) % 2, ct, :], ACT.Identity,
                                                    scale=rstd2[:, ct:ct + 1], bias=shift2[:, ct:ct + 1])
                    last.then_inc(normed_made, 1)

            turns(act, turn)

        @block.vector
        def _(dve):
            def statistics(src, stats, mv, stats_made, mv_made, ready, count):
                for ct in range(CT):
                    ready(ct)
                    last = nc.vector.bn_stats(stats[:, ct, :], src[:, ct, :])
                last.then_inc(stats_made, 1)
                reached_apart(dve, stats_made, count, dve_passed)
                for ct in range(CT):
                    last = nc.vector.bn_aggr(mv[:, ct, :], stats[:, ct, :])
                last.then_inc(mv_made, 1)

            def norm_stats(par, loads, count):
                def ready(ct):
                    if ct == 0:
                        dve.wait_ge(x_loaded[par], loads)
                statistics(xs[:, par], stats1, mv1, stats1_made, mv1_made, ready, count)

            def norm_low(count):
                dve.wait_ge(h1_hi_made, count)
                nc.vector.scalar_tensor_tensor(out=h1_lo[:], in0=normed[:], scalar=0.0, in1=h1_hi[:].bitcast(F32),
                                               op0=ALU.max, op1=ALU.subtract).then_inc(h1_split, 1)

            norm_stats(0, 16, 1)
            norm_low(1)
            dve.wait_ge(exp_made, 2)
            nc.vector.tensor_scalar(gate[:], gate[:], 1.0, None, ALU.add).then_inc(mix_made, 1)
            nc.vector.tensor_scalar(sigma[:], sigma[:], sigma[:, 0:1], -2.0, ALU.mult, ALU.mult).then_inc(mix_made, 1)
            dve.wait_ge(mix_made, 2)
            nc.vector.reciprocal(mix[:, 0:1], gate[:]).then_inc(mix_made, 1)
            nc.vector.reciprocal(neg_rate[:], sigma[:]).then_inc(mix_made, 1)
            dve.wait_ge(mix_made, 4)
            nc.vector.tensor_copy(mix[:, 1:2], mix[:, 0:1])
            nc.vector.tensor_scalar(mix[:, 2:3], mix[:, 0:1], -1.0, 1.0, ALU.mult, ALU.add)
            nc.vector.tensor_scalar(mix[:, 3:4], mix[:, 0:1], -1.0, 1.0, ALU.mult, ALU.add).then_inc(mix_made, 1)
            dve.wait_ge(mix_made, 5)
            nc.vector.tensor_copy(coef[:, 2:4], mix[:, 2:4])
            dve.wait_ge(adj_hi_made, 2)
            low_part(adj_t_lo[:, :, C:C + 2], wqk[:], adj_t_hi[:, :, C:C + 2], adj_lo_made)
            low_part(adj_t_lo[:, :, 0:C], bank[:, 7, :].rearrange("p (t c) -> p t c", t=CT),
                     adj_t_hi[:, :, 0:C], adj_lo_made)
            for k in range(2):
                dve.wait_ge(w_hi_made[k], 1)
                low_part(w_lo[k], w_slot[k], w_hi[k], w_lo_made[k])

            def tri(k):
                dve.wait_ge(tri_hi_made[k], 1)
                for d in range(DT):
                    src = bank[:, 4 * k + d, :]
                    if d:
                        nc.vector.tensor_tensor(tri_lo[:, k, d, 0:d * P], src[:, 0:d * P],
                                                tri_hi[:, k, d, 0:d * P].bitcast(F32), ALU.subtract)
                    own = slice(d * P, (d + 1) * P)
                    last = nc.vector.scalar_tensor_tensor(out=tri_lo[:, k, d, own], in0=src[:, own], scalar=0.5,
                                                          in1=tri_hi[:, k, d, own].bitcast(F32),
                                                          op0=ALU.mult, op1=ALU.subtract)
                last.then_inc(tri_split[k], 1)

            tri(0)
            dve.wait_ge(w_hi_made[2], 1)
            low_part(w_lo[0], w_slot[0], w_hi[0], w_lo_made[2])
            tri(1)
            dve.wait_ge(w_hi_made[3], 1)
            low_part(w_lo[1], bank[:, 0:4, :], w_hi[1], w_lo_made[3])
            dve.wait_ge(wvo_hi_made, 1)
            low_part(wvo_lo[:], bank[:, 4:8, :], wvo_hi[:], wvo_split)
            dve.wait_ge(adj_off_made, 2)

            def turn(i, half):
                has_k, has_b, has_a, has_n = which(i, half)
                k_count, b_count, a_count, n_count = i + half, i + (half + 1), i + (half + 2), i + (half + 3)
                def features_qk(h):
                    dve.wait_ge(ah_hi_made[h], a_count)
                    nc.vector.tensor_copy(qk[:, 2 * h:2 * h + 2, :],
                                          bank[:, 2 * h:2 * h + 2, C:C + 2]).then_inc(qk_copied, 1)

                def features_low(h):
                    low_part(ah_lo[:, 2 * h:2 * h + 2, :], bank[:, 2 * h:2 * h + 2, 0:C],
                             ah_hi[:, 2 * h:2 * h + 2, :], ah_split[h])

                if has_a:
                    features_qk(0)
                    features_low(0)
                if has_k:
                    dve.wait_ge(kt_hi_made, k_count)
                    low_part(kt_lo[:], bank[:, 6, :].rearrange("p (t c) -> p t c", t=CT), kt_hi[:], kt_split)
                if has_b:
                    for h in range(2):
                        dve.wait_ge(ht_hi_made[h], b_count)
                        nc.vector.scalar_tensor_tensor(
                            out=ht_lo[:, 2 * h:2 * h + 2, :],
                            in0=bank[:, 4 + 3 * h, :].rearrange("p (t c) -> p t c", t=2), scalar=0.0,
                            in1=ht_hi[:, 2 * h:2 * h + 2, :].bitcast(F32),
                            op0=ALU.max, op1=ALU.subtract).then_inc(ht_split[h], 1)
                if has_a:
                    features_qk(1)
                    dve.wait_ge(qk_copied, a_count * 2)
                    nc.vector.reduce_max(q_part[:], qk[:, :, 0], AX_X).then_inc(q_part_made, 1)
                    features_low(1)
                if has_a:
                    dve.wait_ge(q_max_made, a_count)
                    nc.vector.tensor_scalar(q_off[:], qk[:, :, 0], q_max[:, 0:1], None, ALU.subtract)
                    nc.vector.tensor_scalar(k_pos[:], qk[:, :, 1], q_max[:, 0:1], 0.0, ALU.add,
                                            ALU.max).then_inc(qk_off_made, 1)

                def t_low(k):
                    for h in range(2):
                        dve.wait_ge(t_hi_made[k][h], b_count)
                        low_part(t_lo[:, k, 2 * h:2 * h + 2, :],
                                 bank[:, 4 + 2 * k + h, :].rearrange("p (t c) -> p t c", t=2),
                                 t_hi[:, k, 2 * h:2 * h + 2, :], t_split[k][h])

                if has_n:
                    norm_stats(half, dma_count(i, half, 2), n_count)
                if has_k:
                    for ct in range(CT):
                        dve.wait_ge(agg_ready[ct], k_count)
                        nc.vector.tensor_tensor(x2[:, 1 - half, ct, :], bank[:, ct, :], x2[:, 1 - half, ct, :],
                                                ALU.add).then_inc(out_made[ct], 1)
                if has_b:
                    t_low(0)
                if has_a:
                    dve.wait_ge(r_rows_copied, a_count)
                    for n in range(DT):
                        last = nc.vector.tensor_scalar(att[:, n, :], r_rows[:], att_c[:, n:n + 1], att_a[:, n:n + 1],
                                                       ALU.mult, ALU.max)
                        if n % 2:
                            last.then_inc(att_made[n // 2], 1)
                if has_b:
                    t_low(1)
                if has_n:
                    norm_low(n_count)
                if has_a:
                    dve.wait_ge(att_hi_made[0], a_count)
                    low_part(att_lo[:, 0:2, :], att[:, 0:2, :], att_hi[:, 0:2, :], att_split[0])
                    dve.wait_ge(att_hi_made[1], a_count)
                    low_part(att_lo[:, 2, :], att[:, 2, :], att_hi[:, 2, :], att_split[1])
                if has_b:
                    for k in range(2):
                        dve.wait_ge(yt_ready[k], b_count)
                        nc.vector.tensor_tensor(gram[:, k], bank[:, 3 + k, :].rearrange("p (t c) -> p t c", t=CT),
                                                ys[:, k], ALU.add).then_inc(gram_made[k], 1)
                    for k in range(2):
                        dve.wait_ge(gram_made[k], b_count)
                        for ct in range(CT):
                            last = nc.vector.scalar_tensor_tensor(
                                out=own[:, 2 * k + ct, :], in0=gram[:, k, ct, ct * P:(ct + 1) * P], scalar=1.0, in1=ident[:],
                                op0=ALU.mult, op1=ALU.mult, accum_out=sq[:, 2 * k + ct:2 * k + ct + 1])
                    last.then_inc(sq_made, 1)
                if has_a:
                    dve.wait_ge(sum_ready, a_count)
                    nc.vector.reciprocal(inv_sum[:], bank[:, 7, :]).then_inc(inv_sum_made, 1)
                    dve.wait_ge(inv_sum_made, a_count)
                    for ct in range(CT):
                        dve.wait_ge(msg_ready[ct], a_count)
                        nc.vector.tensor_tensor(msg[:, ct, :], bank[:, 5 + ct, :], inv_sum[:],
                                                ALU.mult).then_inc(msg_scaled[ct], 1)
                if has_b:
                    dve.wait_ge(rows_ready, b_count)
                    rows = bank[:, 0, :].rearrange("p (k c) -> p k c", k=2)
                    nc.vector.tensor_scalar(g_bias[:], sq[:, 2:4], neg_rate[:, 0:1], None, ALU.mult)
                    nc.vector.scalar_tensor_tensor(
                        out=grav[:], in0=gram[:, 1], scalar=-2.0, in1=rows[:, 1:2, :].to_broadcast([P, CT, C]),
                        op0=ALU.mult, op1=ALU.add).then_inc(dist_made, 1)
                    nc.vector.scalar_tensor_tensor(
                        out=lang[:], in0=gram[:, 0], scalar=0.0, in1=rows[:, 0:1, :].to_broadcast([P, CT, C]),
                        op0=ALU.max, op1=ALU.mult).then_inc(relu_made, 1)
                if has_a:
                    statistics(x2[:, (half + 1) % 2], stats2, mv2, stats2_made, mv2_made,
                               lambda ct: dve.wait_ge(x2_made[ct], a_count), a_count)
                if has_b:
                    dve.wait_ge(relu_made, b_count)
                    for ct in range(CT):
                        last = nc.vector.scalar_tensor_tensor(
                            out=lang[:, ct, :], in0=lang[:, ct, :], scalar=1.0, in1=adj_off[:, ct, :],
                            op0=ALU.mult, op1=ALU.mult, accum_out=deg[:, ct:ct + 1])
                    last.then_inc(lang_made, 1)
                    dve.wait_ge(grav_exp_made, b_count)
                    for ct in range(CT):
                        last = nc.vector.scalar_tensor_tensor(
                            out=grav[:, ct, :], in0=grav[:, ct, :], scalar=1.0, in1=adj_off[:, ct, :],
                            op0=ALU.min, op1=ALU.mult, accum_out=deg[:, 2 + ct:3 + ct])
                    last.then_inc(grav_made, 1)
                    dve.wait_ge(u_hi_made[0], b_count)
                    low_part(u_lo[:, 0, :], bank[:, 1, :], u_hi[:, 0, :], u_split[0])
                if has_b:
                    dve.wait_ge(grav_made, b_count)
                    nc.vector.tensor_tensor(deg[:, 0:2], deg[:, 0:2], cols[:, 0:2], ALU.mult).then_inc(deg_scaled, 1)
                    dve.wait_ge(deg_scaled, b_count)
                    nc.vector.tensor_scalar(deg[:], deg[:], EPS, None, ALU.max).then_inc(deg_clamped, 1)
                    dve.wait_ge(deg_clamped, b_count)
                    nc.vector.tensor_tensor(coef[:, 0:2], mix[:, 0:2], cols[:, 0:2], ALU.mult)
                    nc.vector.reciprocal(deg[:], deg[:]).then_inc(deg_inverted, 1)
                    dve.wait_ge(deg_inverted, b_count)
                    nc.vector.tensor_tensor(deg[:], deg[:], coef[:], ALU.mult).then_inc(deg_mixed, 1)
                    dve.wait_ge(deg_mixed, b_count)
                    for ct in range(CT):
                        last = nc.vector.tensor_scalar(grav[:, ct, :], grav[:, ct, :], deg[:, 2 + ct:3 + ct], None,
                                                       ALU.mult)
                    last.then_inc(grav_scaled, 1)
                    dve.wait_ge(grav_scaled, b_count)
                    for ct in range(CT):
                        last = nc.vector.scalar_tensor_tensor(
                            out=lang[:, ct, :], in0=lang[:, ct, :], scalar=deg[:, ct:ct + 1], in1=grav[:, ct, :],
                            op0=ALU.mult, op1=ALU.add)
                    last.then_inc(k_made, 1)
                    dve.wait_ge(u_hi_made[1], b_count)
                    low_part(u_lo[:, 1, :], bank[:, 2, :], u_hi[:, 1, :], u_split[1])

            turns(dve, turn)

        @block.tensor
        def _(pe):
            def turned(dst, src, done=None):
                last = nc.tensor.transpose(dst, src, ident[:])
                if done is not None:
                    last.then_inc(done, 1)

            pe.wait_ge(ident_made, 2)
            pe.wait_ge(consts_made, 2)
            pe.wait_ge(adj_loaded, 16)
            for c in range(CT):
                for o in range(CT):
                    turned(bank[:, 7, (c * CT + o) * P:(c * CT + o + 1) * P], adj_rows[:, o, c * P:(c + 1) * P],
                           adj_turned if c == o == CT - 1 else None)
            for k in range(2):
                pe.wait_ge(w_lo_made[k], 1)
                if k == 1:
                    pe.wait_ge(adj_lo_made, 2)
                for d in range(DT):
                    last = product(bank[:, 4 * k + d, 0:TRI[d]],
                                   [((w_hi[k][:, t, d * P:(d + 1) * P], w_lo[k][:, t, d * P:(d + 1) * P]),
                                     (w_hi[k][:, t, 0:TRI[d]], w_lo[k][:, t, 0:TRI[d]])) for t in range(DT)])
                last.then_inc(tri_ready[k], 1)
            pe.wait_ge(tri_split[0], 1)
            pe.wait_ge(w_loaded[3], 16)
            for t in range(DT):
                for e in range(DT):
                    turned(bank[:, t, e * P:(e + 1) * P], w_slot[1][:, e, t * P:(t + 1) * P],
                           wo_turned if t == e == DT - 1 else None)
            pe.wait_ge(tri_split[1], 1)
            pe.wait_ge(w_lo_made[2], 1)
            pe.wait_ge(w_lo_made[3], 1)
            for d in range(DT):
                last = product(bank[:, 4 + d, :],
                               [((w_hi[0][:, t, d * P:(d + 1) * P], w_lo[0][:, t, d * P:(d + 1) * P]),
                                 (w_hi[1][:, t, :], w_lo[1][:, t, :])) for t in range(DT)])
            last.then_inc(wvo_ready, 1)
            pe.wait_ge(wvo_split, 1)

            def turn(i, half):
                has_k, has_b, has_a, _ = which(i, half)
                k_count, b_count, a_count = i + half, i + (half + 1), i + (half + 2)
                def features(h):
                    for n in range(2 * h, 2 * h + 2):
                        nodes = slice(n * P, (n + 1) * P)
                        last = product(bank[:, n, 0:C + 2],
                                       [((h1_hi[:, c, nodes], h1_lo[:, c, nodes]),
                                         (adj_t_hi[:, c, :], adj_t_lo[:, c, :])) for c in range(CT)])
                    last.then_inc(ah_ready[h], 1)

                if has_a:
                    pe.wait_ge(h1_split, a_count)
                    if has_k:
                        pe.wait_ge(u_split[0], k_count)
                    features(0)
                if has_k:
                    pe.wait_ge(k_made, k_count)
                    for t in range(CT):
                        for s in range(CT):
                            turned(bank[:, 6, (t * CT + s) * P:(t * CT + s + 1) * P],
                                   lang[:, s, t * P:(t + 1) * P], kt_ready if t == s == CT - 1 else None)
                if has_b:
                    pe.wait_ge(normed_made, b_count)
                    for h in range(2):
                        for s in range(2):
                            d = 2 * h + s
                            for t in range(CT):
                                turned(bank[:, 4 + 3 * h, (s * CT + t) * P:(s * CT + t + 1) * P],
                                       normed[:, t, d * P:(d + 1) * P], ht_ready[h] if s == t == 1 else None)
                if has_a:
                    if has_k:
                        pe.wait_ge(u_split[1], k_count)
                    features(1)
                if has_k:
                    pe.wait_ge(kt_split, k_count)
                    pe.wait_ge(u_split[1], k_count)
                    if has_a:
                        pe.wait_ge(ah_split[0], a_count)
                    for t in range(CT):
                        nodes = slice(t * P, (t + 1) * P)
                        product(bank[:, t, :],
                                [((kt_hi[:, m, nodes], kt_lo[:, m, nodes]),
                                  (u_hi[:, m, :], u_lo[:, m, :])) for m in range(CT)]).then_inc(agg_ready[t], 1)

                def tri_product(k):
                    for h in range(2):
                        for s in range(2):
                            e = 2 * h + s
                            last = product(bank[:, 4 + 2 * k + h, s * C:(s + 1) * C],
                                           [((tri_hi[:, k, d, e * P:(e + 1) * P], tri_lo[:, k, d, e * P:(e + 1) * P]),
                                             (ht_hi[:, d, :], ht_lo[:, d, :])) for d in range(e, DT)])
                        last.then_inc(t_ready[k][h], 1)

                if has_b:
                    for h in range(2):
                        pe.wait_ge(ht_split[h], b_count)
                    tri_product(0)
                def spread(dst, diagonals):
                    nc.tensor.matmul(dst, ones[:], diagonals[:, 4:8, :].rearrange("p t n -> p (t n)"),
                                     start=True, stop=False)
                    return nc.tensor.matmul(dst, ones[:], diagonals[:, 0:4, :].rearrange("p t n -> p (t n)"),
                                            start=False, stop=True)

                if has_a:
                    pe.wait_ge(r_diag_made, a_count)
                    pe.wait_ge(ah_split[1], a_count)
                    spread(bank[:, 2, :], r_diag).then_inc(r_rows_ready, 1)

                def turn_y(k):
                    pe.wait_ge(ys_copied[k], b_count)
                    for t in range(CT):
                        for s in range(CT):
                            turned(bank[:, 3 + k, (t * CT + s) * P:(t * CT + s + 1) * P],
                                   ys[:, k, s, t * P:(t + 1) * P], yt_ready[k] if t == s == CT - 1 else None)

                if has_b:
                    tri_product(1)
                    for k in range(2):
                        for h in range(2):
                            pe.wait_ge(t_split[k][h], b_count)
                        if k == 0 and has_k:
                            pe.wait_ge(out_made[1], k_count)
                        if k == 1 and has_a:
                            pe.wait_ge(r_rows_copied, a_count)
                        for t in range(CT):
                            nodes = slice(t * P, (t + 1) * P)
                            last = product(bank[:, 1 + k, t * C:(t + 1) * C],
                                           [((t_hi[:, k, e, nodes], t_lo[:, k, e, nodes]),
                                             (ht_hi[:, e, :], ht_lo[:, e, :])) for e in range(DT)])
                        last.then_inc(y_ready[k], 1)
                    turn_y(0)
                if has_a:
                    pe.wait_ge(sum_split, a_count)
                    nc.tensor.matmul(bank[:, 7, :], ones[:], sum_lo[:], start=True, stop=False)
                    nc.tensor.matmul(bank[:, 7, :], ones[:], sum_hi[:], start=False, stop=True).then_inc(sum_ready, 1)
                if has_b:
                    turn_y(1)

                def messages(ct):
                    outs = slice(ct * P, (ct + 1) * P)
                    product(bank[:, 5 + ct, :],
                            [((ah_hi[:, n, outs], ah_lo[:, n, outs]),
                              (att_hi[:, n, :], att_lo[:, n, :])) for n in range(DT)]).then_inc(msg_ready[ct], 1)

                if has_a:
                    for h in range(2):
                        pe.wait_ge(att_split[h], a_count)
                    pe.wait_ge(att_tail_split, a_count)
                    messages(0)
                    messages(1)
                if has_b:
                    pe.wait_ge(row_diag_made, b_count)
                    spread(bank[:, 0, :], diag).then_inc(rows_ready, 1)
                    for t in range(CT):
                        nodes = slice(t * P, (t + 1) * P)
                        product(bank[:, 1 + t, :],
                                [((ht_hi[:, d, nodes], ht_lo[:, d, nodes]),
                                  (wvo_hi[:, d, :], wvo_lo[:, d, :])) for d in range(DT)]).then_inc(u_ready[t], 1)

            turns(pe, turn)


_INS = ["x", "adj", "L0_gnn_wq", "L0_gnn_wk", "L0_gnn_bm", "L1_gnn_W_lang", "L1_gnn_W_grav", "L1_gnn_W_V",
        "L1_gnn_W_O", "L1_gnn_gate_logit", "L1_gnn_log_sigma"]


def kernel(**inputs):
    import numpy as _np
    import concourse.bacc as _bacc
    from concourse import mybir as _mybir
    from concourse.bass_utils import run_bass_kernel_spmd as _run

    nc = _bacc.Bacc("TRN2", target_bir_lowering=False, num_devices=1)
    arrays, args = {}, []
    for name in _INS:
        a = _np.ascontiguousarray(inputs[name])
        if a.ndim == 0:
            a = a.reshape(1)
        arrays[f"in_{name}"] = a
        args.append(nc.dram_tensor(f"in_{name}", a.shape, _mybir.dt.from_np(a.dtype), kind="ExternalInput").ap())
    shape = inputs["x"].shape
    args.append(nc.dram_tensor("out_x", shape, _mybir.dt.float32, kind="ExternalOutput").ap())
    program(nc, *args)
    r = _run(nc, [arrays], core_ids=[0])
    return r.results[0]["out_x"]
```

```python
from contextlib import ExitStack

import concourse.bass as bass
from concourse import mybir

P = 128
F32 = mybir.dt.float32
F32R = mybir.dt.float32r
ALU = mybir.AluOpType
ACT = mybir.ActivationFunctionType
AX_X = mybir.AxisListType.X
RMAX = bass.bass_isa.ReduceOp.max

SLOPE = 0.01
LN_EPS = 1e-5
EPS = 1e-8


def reached(eng, semaphore, count):
    if not (isinstance(count, int) and count <= 0):
        eng.wait_ge(semaphore, count)


def reached_apart(eng, semaphore, count, passed):
    eng.wait_ge(semaphore, count)
    if not isinstance(count, int):
        eng.sem_inc(passed, 1)


def program(nc, x, adj, wq, wk, bm, w_lang, w_grav, w_v, w_o, gate_logit, log_sigma, out):
    B, C, D = x.shape
    CT = C // P
    DT = D // P
    TRI = [max((d + 1) * P, 2 * P) for d in range(DT)]
    FOLD_ORDER = (0, 3, 1, 2)
    assert C == 2 * P and D == 4 * P and B % 2 == 0 and B >= 4

    x_v = x.rearrange("b (t p) d -> b p t d", p=P)
    out_v = out.rearrange("b (t p) d -> b p t d", p=P)

    with ExitStack() as ctx:
        def sb(name, shape, dt=F32):
            return ctx.enter_context(nc.sbuf_tensor(name, shape, dt))

        def sem(name):
            return ctx.enter_context(nc.semaphore(name))

        def sems(name, n):
            return [sem(f"{name}_{k}") for k in range(n)]

        ident = sb("ident", [P, P])
        ones = sb("ones", [P, P], F32R)
        minus_half = sb("minus_half", [P, 4])
        adj_rows = sb("adj_rows", [P, CT, C])
        adj_off = sb("adj_off", [P, CT, C])
        wqk = sb("wqk", [P, CT, 2])
        adj_t_hi = sb("adj_t_hi", [P, CT, C + 2], F32R)
        adj_t_lo = sb("adj_t_lo", [P, CT, C + 2], F32R)
        bm_col = sb("bm_col", [P, CT])
        gate = sb("gate", [P, 1])
        sigma = sb("sigma", [P, 1])
        mix = sb("mix", [P, 4])
        neg_rate = sb("neg_rate", [P, 1])
        tri_hi = sb("tri_hi", [P, 2, DT, D], F32R)
        tri_lo = sb("tri_lo", [P, 2, DT, D], F32R)
        wvo_hi = sb("wvo_hi", [P, DT, D], F32R)
        wvo_lo = sb("wvo_lo", [P, DT, D], F32R)

        xs = sb("xs", [P, 2, CT, D])
        x2 = sb("x2", [P, 2, CT, D])
        stats1 = sb("stats1", [P, CT, 6])
        mv1 = sb("mv1", [P, CT, 2])
        var1 = sb("var1", [P, CT])
        rstd1 = sb("rstd1", [P, CT])
        shift1 = sb("shift1", [P, CT])
        normed = sb("normed", [P, CT, D])
        h1_hi = sb("h1_hi", [P, CT, D], F32R)
        h1_lo = sb("h1_lo", [P, CT, D], F32R)
        ah_hi = sb("ah_hi", [P, DT, C], F32R)
        ah_lo = sb("ah_lo", [P, DT, C], F32R)
        qk = sb("qk", [P, DT, 2])
        q_part = sb("q_part", [P, 1])
        q_max = sb("q_max", [P, 1])
        q_off = sb("q_off", [P, DT])
        k_pos = sb("k_pos", [P, DT])
        att_a = sb("att_a", [P, DT])
        att_c = sb("att_c", [P, DT])
        att_r = sb("att_r", [P, DT])
        r_parts = sb("r_parts", [P, 2 * DT], F32R)
        r_diag = sb("r_diag", [P, 2 * DT, P], F32R)
        r_rows = sb("r_rows", [P, D])
        att = sb("att", [P, DT, D])
        att_hi = sb("att_hi", [P, DT, D], F32R)
        att_lo = sb("att_lo", [P, DT, D], F32R)
        att_sum = sb("att_sum", [P, D])
        sum_hi = sb("sum_hi", [P, D], F32R)
        sum_lo = sb("sum_lo", [P, D], F32R)
        inv_sum = sb("inv_sum", [P, D])
        msg = sb("msg", [P, CT, D])
        stats2 = sb("stats2", [P, CT, 6])
        mv2 = sb("mv2", [P, CT, 2])
        var2 = sb("var2", [P, CT])
        rstd2 = sb("rstd2", [P, CT])
        ht_hi = sb("ht_hi", [P, DT, C], F32R)
        ht_lo = sb("ht_lo", [P, DT, C], F32R)
        t_hi = sb("t_hi", [P, 2, DT, C], F32R)
        t_lo = sb("t_lo", [P, 2, DT, C], F32R)
        y_gram = sb("y_gram", [P, 2, 2, CT, C])
        ys, gram = y_gram[:, 0], y_gram[:, 1]
        diag = sb("diag", [P, 8, P], F32R)
        own = sb("own", [P, 4, P])
        cols = sb("cols", [P, 4])
        col_parts = sb("col_parts", [P, 8], F32R)
        coef = sb("coef", [P, 4])
        g_bias = sb("g_bias", [P, CT])
        deg = sb("deg", [P, 4])
        lang_grav = sb("lang_grav", [P, 2, CT, C])
        lang, grav = lang_grav[:, 0], lang_grav[:, 1]
        u_hi = sb("u_hi", [P, CT, D], F32R)
        u_lo = sb("u_lo", [P, CT, D], F32R)
        kt_hi = sb("kt_hi", [P, CT, C], F32R)
        kt_lo = sb("kt_lo", [P, CT, C], F32R)

        bank = ctx.enter_context(nc.psum_tensor("bank", [P, 8, 512], F32))

        def as_weight(buffer):
            return buffer.rearrange("p a (t s) c -> p (a t) (s c)", s=2)

        w_slot = [[y_gram[:, part].rearrange("p k t c -> p k (t c)") for part in range(2)],
                  [lang_grav[:, :, :, :].rearrange("p a t c -> p a (t c)"), x2[:, 1]]]
        w_hi = [as_weight(t_hi[:, :, :, :]), wvo_hi]
        w_lo = [as_weight(t_lo[:, :, :, :]), wvo_lo]

        w_o_hi = [ht_hi[:, :, :].rearrange("p (t s) c -> p t (s c)", s=2), u_hi[:, :, :]]
        w_o_lo = [ht_lo[:, :, :].rearrange("p (t s) c -> p t (s c)", s=2), u_lo[:, :, :]]

        def tri_place(k, d):
            return bank[:, ((4, 4, 5, 6), (0, 0, 1, 3))[k][d], TRI[0] * (d == 1):TRI[0] * (d == 1) + TRI[d]]

        ident_made = sem("ident_made")
        consts_made = sem("consts_made")
        adj_loaded = sem("adj_loaded")
        qk_weights_loaded = sem("qk_weights_loaded")
        small_loaded = sem("small_loaded")
        w_loaded = sems("w_loaded", 4)
        adj_turned = sem("adj_turned")
        adj_hi_made = sem("adj_hi_made")
        adj_lo_made = sem("adj_lo_made")
        adj_off_made = sem("adj_off_made")
        exp_made = sem("exp_made")
        mix_made = sem("mix_made")
        w_hi_made = sems("w_hi_made", 3)
        w_lo_made = sems("w_lo_made", 3)
        wo_turned = sem("wo_turned")
        wo_hi_made = sem("wo_hi_made")
        wo_split = sem("wo_split")
        tri_ready = sems("tri_ready", 2)
        tri_hi_made = sems("tri_hi_made", 2)
        tri_split = sems("tri_split", 2)
        wvo_ready = sem("wvo_ready")
        wvo_hi_made = sem("wvo_hi_made")
        wvo_split = sem("wvo_split")

        dve_passed = sem("dve_passed")
        pool_passed = sem("pool_passed")
        x_loaded = sems("x_loaded", 2)
        stored = sems("stored", 2)
        stats1_made = sem("stats1_made")
        mv1_made = sem("mv1_made")
        var1_made = sem("var1_made")
        rstd1_made = sem("rstd1_made")
        mean1_negated = sem("mean1_negated")
        shift1_made = sem("shift1_made")
        normed1_made = sem("normed1_made")
        h1_hi_made = sems("h1_hi_made", 2)
        h1_split = sem("h1_split")
        ah_ready = sems("ah_ready", 2)
        ah_hi_made = sems("ah_hi_made", 2)
        ah_split = sems("ah_split", 2)
        qk_copied = sem("qk_copied")
        q_part_made = sem("q_part_made")
        q_max_made = sem("q_max_made")
        qk_off_made = sem("qk_off_made")
        r_made = sem("r_made")
        r_split = sem("r_split")
        r_diag_made = sem("r_diag_made")
        r_rows_ready = sem("r_rows_ready")
        r_rows_copied = sem("r_rows_copied")
        att_made = sems("att_made", 2)
        att_hi_made = sems("att_hi_made", 2)
        att_split = sems("att_split", 2)
        att_tail_split = sem("att_tail_split")
        pair_summed = sem("pair_summed")
        three_summed = sem("three_summed")
        att_summed = sem("att_summed")
        sum_hi_made = sem("sum_hi_made")
        sum_split = sem("sum_split")
        sum_ready = sem("sum_ready")
        inv_sum_made = sem("inv_sum_made")
        msg_ready = sems("msg_ready", 2)
        msg_scaled = sems("msg_scaled", 2)
        msg_made = sems("msg_made", 2)
        x2_made = sems("x2_made", 2)
        stats2_made = sem("stats2_made")
        mv2_made = sem("mv2_made")
        var2_made = sem("var2_made")
        rstd2_made = sem("rstd2_made")
        normed_made = sem("normed_made")
        ht_ready = sems("ht_ready", 2)
        ht_hi_made = sems("ht_hi_made", 2)
        ht_split = sems("ht_split", 2)
        t_ready = [sems(f"t_ready_{k}", 2) for k in range(2)]
        t_hi_made = [sems(f"t_hi_made_{k}", 2) for k in range(2)]
        t_split = [sems(f"t_split_{k}", 2) for k in range(2)]
        y_ready = sems("y_ready", 2)
        ys_copied = sems("ys_copied", 2)
        yt_ready = sems("yt_ready", 2)
        gram_made = sems("gram_made", 2)
        sq_made = sem("sq_made")
        len_clamped = sem("len_clamped")
        cols_made = sem("cols_made")
        cols_hi_made = sem("cols_hi_made")
        cols_split = sem("cols_split")
        row_diag_made = sems("row_diag_made", 2)
        rows_ready = sem("rows_ready")
        relu_made = sem("relu_made")
        dist_made = sem("dist_made")
        lang_made = sem("lang_made")
        grav_exp_made = sem("grav_exp_made")
        grav_made = sem("grav_made")
        deg_scaled = sem("deg_scaled")
        deg_clamped = sem("deg_clamped")
        deg_inverted = sem("deg_inverted")
        deg_mixed = sem("deg_mixed")
        grav_scaled = sem("grav_scaled")
        k_made = sem("k_made")
        u_ready = sems("u_ready", 2)
        u_copied = sems("u_copied", 2)
        u_split = sems("u_split", 2)
        kt_ready = sem("kt_ready")
        kt_hi_made = sem("kt_hi_made")
        kt_split = sem("kt_split")
        agg_ready = sems("agg_ready", 2)
        out_made = sems("out_made", 2)

        def low_part(lo, full, hi, done):
            nc.vector.tensor_tensor(lo, full, hi.bitcast(F32), ALU.subtract).then_inc(done, 1)

        def product(dst, pairs, begins=True, ends=True):
            for n, ((lhs_hi, lhs_lo), (rhs_hi, rhs_lo)) in enumerate(pairs):
                nc.tensor.matmul(dst, lhs_lo, rhs_hi, start=(begins and n == 0), stop=False)
                nc.tensor.matmul(dst, lhs_hi, rhs_lo, start=False, stop=False)
                last = nc.tensor.matmul(dst, lhs_hi, rhs_hi, start=False, stop=(ends and n == len(pairs) - 1))
            return last

        def turns(eng, turn):
            turn(-2, 1)
            turn(0, 0)
            turn(0, 1)
            with eng.Fori(2, B - 3, 2) as i:
                turn(i, 0)
                turn(i, 1)
            turn(B - 2, 0)
            turn(B - 2, 1)
            turn(B, 0)

        def which(i, half):
            if not isinstance(i, int):
                return True, True, True, True
            return tuple(0 <= i + half + ahead < B for ahead in (-1, 0, 1, 2))

        def opens(i):
            return isinstance(i, int) and i < 0

        def dma_count(i, half, ahead):
            return i * 8 + 16 * ((half + ahead) // 2 + 1)

        block = ctx.enter_context(nc.Block())

        @block.sync
        def _(sp):
            sp.dma_start(xs[:, 0], x_v[0]).then_inc(x_loaded[0], 16)
            sp.dma_start(adj_rows[:], adj.rearrange("(t p) c -> p t c", p=P)).then_inc(adj_loaded, 16)
            def load_weight(k, weight):
                rows = weight.rearrange("(a t p) d -> a p t d", a=2, p=P)
                for part in range(2):
                    sp.dma_start(w_slot[k % 2][part], rows[part]).then_inc(w_loaded[k], 16)

            load_weight(0, w_lang)
            load_weight(1, w_grav)
            sp.dma_start(xs[:, 1], x_v[1]).then_inc(x_loaded[1], 16)
            sp.wait_ge(w_lo_made[0], 2)
            load_weight(2, w_v)
            sp.wait_ge(w_lo_made[1], 2)
            load_weight(3, w_o)

            def turn(i, half):
                has_k, has_b, _, has_n = which(i, half)
                if has_b and has_n:
                    for ct in range(CT):
                        sp.wait_ge(x2_made[ct], i + (half + 1))
                    sp.dma_start(xs[:, half], x_v[i + (half + 2)]).then_inc(x_loaded[half], 16)
                if has_k and has_b:
                    for ct in range(CT):
                        sp.wait_ge(out_made[ct], i + half)
                    sp.dma_start(out_v[i + (half - 1)], x2[:, 1 - half]).then_inc(stored[1 - half], 16)
                elif has_k:
                    for ct in range(CT):
                        sp.wait_ge(out_made[ct], B)
                        sp.dma_start(out_v[B - 1, :, ct], x2[:, 1, ct]).then_inc(stored[1], 16)

            turns(sp, turn)
            sp.wait_ge(stored[0], 16 * (B // 2))
            sp.wait_ge(stored[1], 16 * (B // 2 + 1))

        @block.gpsimd
        def _(pool):
            nc.gpsimd.memset(ident[:], 0.0).then_inc(ident_made, 1)
            nc.gpsimd.memset(ones[:].bitcast(F32), 1.0).then_inc(consts_made, 1)
            nc.gpsimd.memset(minus_half[:], -0.5).then_inc(consts_made, 1)
            pool.wait_ge(ident_made, 1)
            nc.gpsimd.affine_select(out=ident[:], in_=ident[:], compare_op=ALU.not_equal, fill=1.0, base=0,
                                    pattern=[[-1, P]], channel_multiplier=1).then_inc(ident_made, 1)
            pool.wait_ge(consts_made, 2)
            pool.wait_ge(adj_loaded, 16)
            for t in range(CT):
                nc.gpsimd.affine_select(out=adj_off[:, t, :], in_=adj_rows[:, t, :], compare_op=ALU.not_equal,
                                        fill=0.0, base=P * t, pattern=[[-1, C]],
                                        channel_multiplier=1).then_inc(adj_off_made, 1)

            def inverse_deviation(mv, var, rstd, mv_made, var_made, rstd_made, count):
                reached_apart(pool, mv_made, count, pool_passed)
                nc.gpsimd.tensor_scalar(var[:], mv[:, :, 1], LN_EPS, 1.0, ALU.add, ALU.mult).then_inc(var_made, 1)
                pool.wait_ge(var_made, count)
                nc.gpsimd.tensor_tensor(rstd[:], var[:], minus_half[:, 0:CT], ALU.pow).then_inc(rstd_made, 1)

            def norm_terms(count):
                inverse_deviation(mv1, var1, rstd1, mv1_made, var1_made, rstd1_made, count)
                nc.gpsimd.tensor_scalar(shift1[:], mv1[:, :, 0], -1.0, 0.0, ALU.mult, ALU.add).then_inc(mean1_negated, 1)
                pool.wait_ge(rstd1_made, count)
                pool.wait_ge(mean1_negated, count)
                nc.gpsimd.tensor_tensor(shift1[:], shift1[:], rstd1[:], ALU.mult).then_inc(shift1_made, 1)

            def norm_low(count):
                for ct in range(CT):
                    pool.wait_ge(h1_hi_made[ct], count)
                    last = nc.gpsimd.tensor_tensor(h1_lo[:, ct, :], normed[:, ct, :], h1_hi[:, ct, :].bitcast(F32),
                                                   ALU.subtract)
                last.then_inc(h1_split, 1)

            norm_terms(1)

            def turn(i, half):
                _, has_b, has_a, has_n = which(i, half)
                b_count, a_count, n_count = i + (half + 1), i + (half + 2), i + (half + 3)
                if has_a:
                    reached_apart(pool, q_part_made, a_count, pool_passed)
                    nc.gpsimd.partition_all_reduce(q_max[:], q_part[:], P, RMAX).then_inc(q_max_made, 1)
                    pool.wait_ge(r_made, a_count)
                    nc.gpsimd.tensor_tensor(r_parts[:, DT:2 * DT], att_r[:], r_parts[:, 0:DT].bitcast(F32),
                                            ALU.subtract).then_inc(r_split, 1)
                    pool.wait_ge(r_split, a_count)
                    nc.gpsimd.tensor_tensor(r_diag[:], ident[:, None, :].to_broadcast([P, 2 * DT, P]),
                                            r_parts[:, :, None].bitcast(F32).to_broadcast([P, 2 * DT, P]),
                                            ALU.mult).then_inc(r_diag_made, 1)
                    pool.wait_ge(att_made[0], a_count)
                    nc.gpsimd.tensor_tensor(att_sum[:], att[:, 0, :], att[:, 1, :], ALU.add).then_inc(pair_summed, 1)
                    pool.wait_ge(att_made[1], a_count)
                    pool.wait_ge(pair_summed, a_count)
                    nc.gpsimd.tensor_tensor(att_sum[:], att_sum[:], att[:, 2, :], ALU.add).then_inc(three_summed, 1)
                    pool.wait_ge(three_summed, a_count)
                    nc.gpsimd.tensor_tensor(att_sum[:], att_sum[:], att[:, 3, :], ALU.add).then_inc(att_summed, 1)
                    pool.wait_ge(sum_hi_made, a_count)
                    nc.gpsimd.tensor_tensor(sum_lo[:], att_sum[:], sum_hi[:].bitcast(F32),
                                            ALU.subtract).then_inc(sum_split, 1)
                if has_n:
                    norm_terms(n_count)
                if has_a:
                    pool.wait_ge(att_hi_made[1], a_count)
                    nc.gpsimd.tensor_tensor(att_lo[:, 3, :], att[:, 3, :], att_hi[:, 3, :].bitcast(F32),
                                            ALU.subtract).then_inc(att_tail_split, 1)
                if has_b:
                    reached_apart(pool, sq_made, b_count, pool_passed)
                    nc.gpsimd.tensor_scalar(cols[:, 0:2], cols[:, 0:2], EPS * EPS, 0.0, ALU.max,
                                            ALU.add).then_inc(len_clamped, 1)
                    pool.wait_ge(len_clamped, b_count)
                    nc.gpsimd.tensor_tensor(cols[:, 0:2], cols[:, 0:2], minus_half[:, 0:2],
                                            ALU.pow).then_inc(cols_made, 1)
                    pool.wait_ge(cols_made, b_count)
                    nc.gpsimd.tensor_tensor(col_parts[:, 0:4], cols[:], ones[:, 0:4].bitcast(F32),
                                            ALU.mult).then_inc(cols_hi_made, 1)
                    pool.wait_ge(cols_hi_made, b_count)
                    nc.gpsimd.tensor_tensor(col_parts[:, 4:8], cols[:], col_parts[:, 0:4].bitcast(F32),
                                            ALU.subtract).then_inc(cols_split, 1)
                    pool.wait_ge(cols_split, b_count)
                    nc.gpsimd.tensor_tensor(diag[:, 4:8, :], ident[:, None, :].to_broadcast([P, 4, P]),
                                            col_parts[:, 4:8, None].bitcast(F32).to_broadcast([P, 4, P]),
                                            ALU.mult).then_inc(row_diag_made[1], 1)
                if has_a:
                    par = (half + 1) % 2
                    pool.wait_ge(msg_made[0], a_count)
                    reached(pool, stored[par], dma_count(i, half, -1))
                    nc.gpsimd.tensor_tensor(x2[:, par, 0, :], xs[:, par, 0, :], msg[:, 0, :],
                                            ALU.add).then_inc(x2_made[0], 1)
                if has_n:
                    norm_low(n_count)
                if has_a:
                    inverse_deviation(mv2, var2, rstd2, mv2_made, var2_made, rstd2_made, a_count)
                if has_b:
                    for ct in range(CT):
                        pool.wait_ge(u_copied[ct], b_count)
                        nc.gpsimd.tensor_tensor(u_lo[:, ct, :], msg[:, ct, :], u_hi[:, ct, :].bitcast(F32),
                                                ALU.subtract).then_inc(u_split[ct], 1)

            turns(pool, turn)

        @block.scalar
        def _(act):
            act.dma_start(wqk[:, :, 0], wq.rearrange("(t p) -> p t", p=P),
                          allow_slow_non_contiguous=True).then_inc(qk_weights_loaded, 16)
            act.dma_start(wqk[:, :, 1], wk.rearrange("(t p) -> p t", p=P),
                          allow_slow_non_contiguous=True).then_inc(qk_weights_loaded, 16)
            act.dma_start(bm_col[:], bm.rearrange("(t p) -> p t", p=P),
                          allow_slow_non_contiguous=True).then_inc(small_loaded, 16)
            act.dma_start(gate[:], gate_logit.partition_broadcast(P)).then_inc(small_loaded, 16)
            act.dma_start(sigma[:], log_sigma.partition_broadcast(P)).then_inc(small_loaded, 16)
            def norm_relu(par, count):
                act.wait_ge(shift1_made, count)
                for ct in range(CT):
                    last = nc.scalar.activation(normed[:, ct, :], xs[:, par, ct, :], ACT.Relu,
                                                scale=rstd1[:, ct:ct + 1], bias=shift1[:, ct:ct + 1])
                last.then_inc(normed1_made, 1)

            def norm_high(ct, count):
                act.wait_ge(normed1_made, count)
                nc.scalar.activation(h1_hi[:, ct, :], normed[:, ct, :], ACT.Copy).then_inc(h1_hi_made[ct], 1)

            act.wait_ge(adj_turned, 1)
            nc.scalar.activation(adj_t_hi[:, :, 0:C], bank[:, 7, :].rearrange("p (t c) -> p t c", t=CT),
                                 ACT.Copy).then_inc(adj_hi_made, 1)
            norm_relu(0, 1)
            for ct in range(CT):
                norm_high(ct, 1)
            act.wait_ge(qk_weights_loaded, 32)
            nc.scalar.activation(adj_t_hi[:, :, C:C + 2], wqk[:], ACT.Copy).then_inc(adj_hi_made, 1)

            def weight_high(k):
                act.wait_ge(w_loaded[k], 32)
                for part in range(2):
                    nc.scalar.activation(w_hi[k % 2][:, 2 * part:2 * part + 2, :], w_slot[k % 2][part],
                                         ACT.Copy).then_inc(w_hi_made[k], 1)

            def tri_high(k):
                act.wait_ge(tri_ready[k], 1)
                for d in range(DT):
                    src = tri_place(k, d)
                    if d:
                        nc.scalar.activation(tri_hi[:, k, d, 0:d * P], src[:, 0:d * P], ACT.Copy)
                    last = nc.scalar.activation(tri_hi[:, k, d, d * P:(d + 1) * P], src[:, d * P:(d + 1) * P],
                                                ACT.Copy, scale=0.5)
                last.then_inc(tri_hi_made[k], 1)

            weight_high(0)
            act.wait_ge(small_loaded, 48)
            nc.scalar.activation(gate[:], gate[:], ACT.Exp, scale=-1.0).then_inc(exp_made, 1)
            nc.scalar.activation(sigma[:], sigma[:], ACT.Exp).then_inc(exp_made, 1)
            weight_high(1)

            def turn(i, half):
                has_k, has_b, has_a, has_n = which(i, half)
                k_count, b_count, a_count, n_count = i + half, i + (half + 1), i + (half + 2), i + (half + 3)
                def features_high(h):
                    act.wait_ge(ah_ready[h], a_count)
                    if h == 1:
                        act.wait_ge(qk_copied, a_count * 2)
                    nc.scalar.activation(ah_hi[:, 2 * h:2 * h + 2, :], bank[:, 2 * h:2 * h + 2, 0:C],
                                         ACT.Copy).then_inc(ah_hi_made[h], 1)

                if has_a:
                    features_high(0)
                if has_b:
                    for h in (1, 0):
                        act.wait_ge(ht_ready[h], b_count)
                        nc.scalar.activation(ht_hi[:, 2 * h:2 * h + 2, :],
                                             bank[:, 4 + 3 * h, :].rearrange("p (t c) -> p t c", t=2),
                                             ACT.Relu).then_inc(ht_hi_made[h], 1)
                if has_a:
                    features_high(1)
                if has_a:
                    act.wait_ge(qk_off_made, a_count)
                    nc.scalar.activation(att_r[:], k_pos[:], ACT.Exp, scale=SLOPE - 1.0)
                    nc.scalar.activation(r_parts[:, 0:DT], k_pos[:], ACT.Exp, scale=SLOPE - 1.0).then_inc(r_made, 1)
                    nc.scalar.activation(att_a[:], q_off[:], ACT.Exp)
                    nc.scalar.activation(att_c[:], q_off[:], ACT.Exp, scale=SLOPE)

                def t_high(k, h):
                    act.wait_ge(t_ready[k][h], b_count)
                    nc.scalar.activation(t_hi[:, k, 2 * h:2 * h + 2, :],
                                         bank[:, 4 + 2 * k + h, :].rearrange("p (t c) -> p t c", t=2),
                                         ACT.Copy).then_inc(t_hi_made[k][h], 1)

                def copy_y(k):
                    act.wait_ge(y_ready[k], b_count)
                    nc.scalar.activation(ys[:, k], bank[:, 1 + k, :].rearrange("p (t c) -> p t c", t=CT),
                                         ACT.Copy).then_inc(ys_copied[k], 1)

                if has_b:
                    t_high(0, 1)
                if has_k:
                    act.wait_ge(kt_ready, k_count)
                    nc.scalar.activation(kt_hi[:], bank[:, 6, :].rearrange("p (t c) -> p t c", t=CT),
                                         ACT.Copy).then_inc(kt_hi_made, 1)
                if has_b:
                    t_high(0, 0)
                if has_a:
                    act.wait_ge(r_rows_ready, a_count)
                    nc.scalar.activation(r_rows[:], bank[:, 2, :], ACT.Copy).then_inc(r_rows_copied, 1)
                if opens(i):
                    tri_high(0)
                if has_b:
                    t_high(1, 1)
                if has_a:
                    for h in range(2):
                        act.wait_ge(att_made[h], a_count)
                        nc.scalar.activation(att_hi[:, 2 * h:2 * h + 2, :], att[:, 2 * h:2 * h + 2, :],
                                             ACT.Copy).then_inc(att_hi_made[h], 1)
                if has_b:
                    t_high(1, 0)
                if opens(i):
                    weight_high(2)
                if has_a:
                    act.wait_ge(att_summed, a_count)
                    nc.scalar.activation(sum_hi[:], att_sum[:], ACT.Copy).then_inc(sum_hi_made, 1)
                if opens(i):
                    tri_high(1)
                if has_b:
                    copy_y(0)
                y_first = has_b and not has_k
                if y_first:
                    copy_y(1)
                if has_n:
                    norm_relu(half, n_count)
                if has_b and not y_first:
                    copy_y(1)
                if has_n:
                    for ct in range(CT):
                        norm_high(ct, n_count)
                if opens(i):
                    for t in range(DT):
                        act.wait_ge(wo_turned, t + 1)
                        nc.scalar.activation(w_o_hi[t // 2][:, t % 2, :], bank[:, t, :], ACT.Copy).then_inc(wo_hi_made, 1)
                if has_a:
                    for ct in range(CT):
                        act.wait_ge(msg_scaled[ct], a_count)
                        nc.scalar.activation(msg[:, ct, :], msg[:, ct, :], ACT.Relu,
                                             bias=bm_col[:, ct:ct + 1]).then_inc(msg_made[ct], 1)
                if has_b:
                    act.wait_ge(dist_made, b_count)
                    for t in range(CT):
                        last = nc.scalar.activation(grav[:, t, :], grav[:, t, :], ACT.Exp,
                                                    scale=neg_rate[:, 0:1], bias=g_bias[:, t:t + 1])
                    last.then_inc(grav_exp_made, 1)
                    for ct in range(CT):
                        act.wait_ge(u_ready[ct], b_count)
                        nc.scalar.activation(u_hi[:, ct, :], bank[:, 1 + ct, :], ACT.Copy)
                        if has_a:
                            act.wait_ge(x2_made[ct], a_count)
                        nc.scalar.activation(msg[:, ct, :], bank[:, 1 + ct, :], ACT.Copy).then_inc(u_copied[ct], 1)
                if opens(i):
                    for n, d in enumerate(FOLD_ORDER):
                        act.wait_ge(wvo_ready, n + 1)
                        nc.scalar.activation(wvo_hi[:, d, :], bank[:, 4 + d, :], ACT.Copy).then_inc(wvo_hi_made, 1)

            turns(act, turn)

        @block.vector
        def _(dve):
            def statistics(src, stats, stats_made, ready):
                for ct in range(CT):
                    ready(ct)
                    last = nc.vector.bn_stats(stats[:, ct, :], src[:, ct, :])
                last.then_inc(stats_made, 1)

            def aggregate(stats, mv, stats_made, mv_made, count):
                reached_apart(dve, stats_made, count, dve_passed)
                for ct in range(CT):
                    last = nc.vector.bn_aggr(mv[:, ct, :], stats[:, ct, :])
                last.then_inc(mv_made, 1)

            def norm_stats(par, loads):
                def ready(ct):
                    if ct == 0:
                        dve.wait_ge(x_loaded[par], loads)
                statistics(xs[:, par], stats1, stats1_made, ready)

            norm_stats(0, 16)
            aggregate(stats1, mv1, stats1_made, mv1_made, 1)
            dve.wait_ge(adj_hi_made, 1)
            low_part(adj_t_lo[:, :, 0:C], bank[:, 7, :].rearrange("p (t c) -> p t c", t=CT),
                     adj_t_hi[:, :, 0:C], adj_lo_made)
            dve.wait_ge(h1_hi_made[0], 1)
            nc.vector.tensor_tensor(h1_lo[:, 0, :], normed[:, 0, :], h1_hi[:, 0, :].bitcast(F32), ALU.subtract)
            dve.wait_ge(h1_hi_made[1], 1)
            low_part(h1_lo[:, 1, :], normed[:, 1, :], h1_hi[:, 1, :], h1_split)
            dve.wait_ge(adj_hi_made, 2)
            low_part(adj_t_lo[:, :, C:C + 2], wqk[:], adj_t_hi[:, :, C:C + 2], adj_lo_made)

            def weight_low(k):
                for part in range(2):
                    rows = slice(2 * part, 2 * part + 2)
                    dve.wait_ge(w_hi_made[k], part + 1)
                    low_part(w_lo[k % 2][:, rows, :], w_slot[k % 2][part], w_hi[k % 2][:, rows, :], w_lo_made[k])

            def tri_low(k):
                dve.wait_ge(tri_hi_made[k], 1)
                for d in range(DT):
                    src = tri_place(k, d)
                    if d:
                        nc.vector.tensor_tensor(tri_lo[:, k, d, 0:d * P], src[:, 0:d * P],
                                                tri_hi[:, k, d, 0:d * P].bitcast(F32), ALU.subtract)
                    own_block = slice(d * P, (d + 1) * P)
                    last = nc.vector.scalar_tensor_tensor(out=tri_lo[:, k, d, own_block], in0=src[:, own_block],
                                                          scalar=0.5, in1=tri_hi[:, k, d, own_block].bitcast(F32),
                                                          op0=ALU.mult, op1=ALU.subtract)
                last.then_inc(tri_split[k], 1)

            weight_low(0)
            dve.wait_ge(exp_made, 2)
            nc.vector.tensor_scalar(gate[:], gate[:], 1.0, None, ALU.add).then_inc(mix_made, 1)
            nc.vector.tensor_scalar(sigma[:], sigma[:], sigma[:, 0:1], -2.0, ALU.mult, ALU.mult).then_inc(mix_made, 1)
            dve.wait_ge(mix_made, 2)
            nc.vector.reciprocal(mix[:, 0:1], gate[:]).then_inc(mix_made, 1)
            nc.vector.reciprocal(neg_rate[:], sigma[:]).then_inc(mix_made, 1)
            dve.wait_ge(mix_made, 4)
            nc.vector.tensor_copy(mix[:, 1:2], mix[:, 0:1])
            nc.vector.tensor_scalar(mix[:, 2:3], mix[:, 0:1], -1.0, 1.0, ALU.mult, ALU.add)
            nc.vector.tensor_scalar(mix[:, 3:4], mix[:, 0:1], -1.0, 1.0, ALU.mult, ALU.add).then_inc(mix_made, 1)
            dve.wait_ge(mix_made, 5)
            nc.vector.tensor_copy(coef[:, 2:4], mix[:, 2:4])
            dve.wait_ge(adj_off_made, 2)

            def turn(i, half):
                has_k, has_b, has_a, has_n = which(i, half)
                k_count, b_count, a_count, n_count = i + half, i + (half + 1), i + (half + 2), i + (half + 3)
                def features_qk(h):
                    dve.wait_ge(ah_ready[1] if h else ah_hi_made[0], a_count)
                    nc.vector.tensor_copy(qk[:, 2 * h:2 * h + 2, :],
                                          bank[:, 2 * h:2 * h + 2, C:C + 2]).then_inc(qk_copied, 1)

                def features_low(h):
                    if h == 1:
                        dve.wait_ge(ah_hi_made[1], a_count)
                    low_part(ah_lo[:, 2 * h:2 * h + 2, :], bank[:, 2 * h:2 * h + 2, 0:C],
                             ah_hi[:, 2 * h:2 * h + 2, :], ah_split[h])

                if has_k:
                    dve.wait_ge(grav_made, k_count)
                    nc.vector.tensor_tensor(deg[:, 0:2], deg[:, 0:2], cols[:, 0:2], ALU.mult).then_inc(deg_scaled, 1)
                    dve.wait_ge(deg_scaled, k_count)
                    nc.vector.tensor_scalar(deg[:], deg[:], EPS, None, ALU.max).then_inc(deg_clamped, 1)
                    dve.wait_ge(deg_clamped, k_count)
                    nc.vector.tensor_tensor(coef[:, 0:2], mix[:, 0:2], cols[:, 0:2], ALU.mult)
                    nc.vector.reciprocal(deg[:], deg[:]).then_inc(deg_inverted, 1)
                def nodes_low(h):
                    dve.wait_ge(ht_hi_made[h], b_count)
                    nc.vector.scalar_tensor_tensor(
                        out=ht_lo[:, 2 * h:2 * h + 2, :],
                        in0=bank[:, 4 + 3 * h, :].rearrange("p (t c) -> p t c", t=2), scalar=0.0,
                        in1=ht_hi[:, 2 * h:2 * h + 2, :].bitcast(F32),
                        op0=ALU.max, op1=ALU.subtract).then_inc(ht_split[h], 1)

                if has_b:
                    nodes_low(1)
                if has_a:
                    features_qk(0)
                if has_k:
                    dve.wait_ge(deg_inverted, k_count)
                    nc.vector.tensor_tensor(deg[:], deg[:], coef[:], ALU.mult).then_inc(deg_mixed, 1)
                if has_b:
                    nodes_low(0)
                if has_a:
                    features_qk(1)
                    dve.wait_ge(qk_copied, a_count * 2)
                    nc.vector.reduce_max(q_part[:], qk[:, :, 0], AX_X).then_inc(q_part_made, 1)
                if has_k:
                    dve.wait_ge(deg_mixed, k_count)
                    for ct in range(CT):
                        last = nc.vector.tensor_scalar(grav[:, ct, :], grav[:, ct, :], deg[:, 2 + ct:3 + ct], None,
                                                       ALU.mult)
                    last.then_inc(grav_scaled, 1)
                if has_a:
                    dve.wait_ge(q_max_made, a_count)
                    nc.vector.tensor_scalar(q_off[:], qk[:, :, 0], q_max[:, 0:1], None, ALU.subtract)
                    nc.vector.tensor_scalar(k_pos[:], qk[:, :, 1], q_max[:, 0:1], 0.0, ALU.add,
                                            ALU.max).then_inc(qk_off_made, 1)
                if has_k:
                    dve.wait_ge(grav_scaled, k_count)
                    for ct in range(CT):
                        last = nc.vector.scalar_tensor_tensor(
                            out=lang[:, ct, :], in0=lang[:, ct, :], scalar=deg[:, ct:ct + 1], in1=grav[:, ct, :],
                            op0=ALU.mult, op1=ALU.add)
                    last.then_inc(k_made, 1)
                if has_a:
                    features_low(0)
                    features_low(1)
                if opens(i):
                    weight_low(1)

                def t_low(k, h):
                    dve.wait_ge(t_hi_made[k][h], b_count)
                    low_part(t_lo[:, k, 2 * h:2 * h + 2, :],
                             bank[:, 4 + 2 * k + h, :].rearrange("p (t c) -> p t c", t=2),
                             t_hi[:, k, 2 * h:2 * h + 2, :], t_split[k][h])

                if has_b:
                    t_low(0, 1)
                if has_k:
                    dve.wait_ge(kt_hi_made, k_count)
                    low_part(kt_lo[:], bank[:, 6, :].rearrange("p (t c) -> p t c", t=CT), kt_hi[:], kt_split)
                if has_b:
                    t_low(0, 0)
                if has_a:
                    dve.wait_ge(r_rows_copied, a_count)
                    for n in range(DT):
                        last = nc.vector.tensor_scalar(att[:, n, :], r_rows[:], att_c[:, n:n + 1], att_a[:, n:n + 1],
                                                       ALU.mult, ALU.max)
                        if n % 2:
                            last.then_inc(att_made[n // 2], 1)
                if opens(i):
                    tri_low(0)
                if has_b:
                    t_low(1, 1)
                k_late = has_k and has_b and not has_a

                def add_residual():
                    for ct in range(CT):
                        dve.wait_ge(agg_ready[ct], k_count)
                        nc.vector.tensor_tensor(x2[:, 1 - half, ct, :], bank[:, ct, :], x2[:, 1 - half, ct, :],
                                                ALU.add).then_inc(out_made[ct], 1)

                if has_k and not k_late:
                    add_residual()
                if has_a:
                    dve.wait_ge(att_hi_made[0], a_count)
                    low_part(att_lo[:, 0:2, :], att[:, 0:2, :], att_hi[:, 0:2, :], att_split[0])
                if has_b:
                    t_low(1, 0)
                if has_n:
                    norm_stats(half, dma_count(i, half, 2))
                    aggregate(stats1, mv1, stats1_made, mv1_made, n_count)
                if has_a:
                    dve.wait_ge(att_hi_made[1], a_count)
                    low_part(att_lo[:, 2, :], att[:, 2, :], att_hi[:, 2, :], att_split[1])
                    if opens(i):
                        weight_low(2)
                        tri_low(1)
                        for t in range(DT):
                            dve.wait_ge(wo_hi_made, t + 1)
                            low_part(w_o_lo[t // 2][:, t % 2, :], bank[:, t, :], w_o_hi[t // 2][:, t % 2, :],
                                     wo_split)
                    dve.wait_ge(sum_ready, a_count)
                    nc.vector.reciprocal(inv_sum[:], bank[:, 7, :]).then_inc(inv_sum_made, 1)
                def scale_messages(ct):
                    dve.wait_ge(msg_ready[ct], a_count)
                    nc.vector.tensor_tensor(msg[:, ct, :], bank[:, 5 + ct, :], inv_sum[:],
                                            ALU.mult).then_inc(msg_scaled[ct], 1)

                if has_b:
                    for k in range(2):
                        dve.wait_ge(yt_ready[k], b_count)
                        nc.vector.tensor_tensor(gram[:, k], bank[:, 3 + k, :].rearrange("p (t c) -> p t c", t=CT),
                                                ys[:, k], ALU.add).then_inc(gram_made[k], 1)
                    for k in range(2):
                        dve.wait_ge(gram_made[k], b_count)
                        for ct in range(CT):
                            last = nc.vector.scalar_tensor_tensor(
                                out=own[:, 2 * k + ct, :], in0=gram[:, k, ct, ct * P:(ct + 1) * P], scalar=1.0, in1=ident[:],
                                op0=ALU.mult, op1=ALU.mult, accum_out=cols[:, 2 * k + ct:2 * k + ct + 1])
                    last.then_inc(sq_made, 1)
                if has_a:
                    dve.wait_ge(inv_sum_made, a_count)
                    scale_messages(0)
                if has_b:
                    if k_late:
                        add_residual()
                    dve.wait_ge(cols_hi_made, b_count)
                    nc.vector.tensor_tensor(diag[:, 0:4, :], ident[:, None, :].to_broadcast([P, 4, P]),
                                            col_parts[:, 0:4, None].bitcast(F32).to_broadcast([P, 4, P]),
                                            ALU.mult).then_inc(row_diag_made[0], 1)
                if has_a:
                    scale_messages(1)
                if has_b:
                    dve.wait_ge(rows_ready, b_count)
                    rows = bank[:, 0, :].rearrange("p (k c) -> p k c", k=2)
                    nc.vector.tensor_scalar(g_bias[:], cols[:, 2:4], neg_rate[:, 0:1], None, ALU.mult)
                    nc.vector.scalar_tensor_tensor(
                        out=grav[:], in0=gram[:, 1], scalar=-2.0, in1=rows[:, 1:2, :].to_broadcast([P, CT, C]),
                        op0=ALU.mult, op1=ALU.add).then_inc(dist_made, 1)
                if has_a:
                    par = (half + 1) % 2
                    dve.wait_ge(msg_made[1], a_count)
                    reached(dve, stored[par], dma_count(i, half, -1))
                    nc.vector.tensor_tensor(x2[:, par, 1, :], xs[:, par, 1, :], msg[:, 1, :],
                                            ALU.add).then_inc(x2_made[1], 1)
                    statistics(x2[:, par], stats2, stats2_made, lambda ct: dve.wait_ge(x2_made[ct], a_count))
                    aggregate(stats2, mv2, stats2_made, mv2_made, a_count)
                if has_b:
                    nc.vector.scalar_tensor_tensor(
                        out=lang[:], in0=gram[:, 0], scalar=0.0, in1=rows[:, 0:1, :].to_broadcast([P, CT, C]),
                        op0=ALU.max, op1=ALU.mult).then_inc(relu_made, 1)
                if has_a:
                    dve.wait_ge(rstd2_made, a_count)
                    for ct in range(CT):
                        last = nc.vector.tensor_scalar(normed[:, ct, :], x2[:, par, ct, :], mv2[:, ct, 0:1],
                                                       rstd2[:, ct:ct + 1], ALU.subtract, ALU.mult)
                    last.then_inc(normed_made, 1)
                if has_b:
                    dve.wait_ge(relu_made, b_count)
                    for ct in range(CT):
                        last = nc.vector.scalar_tensor_tensor(
                            out=lang[:, ct, :], in0=lang[:, ct, :], scalar=1.0, in1=adj_off[:, ct, :],
                            op0=ALU.mult, op1=ALU.mult, accum_out=deg[:, ct:ct + 1])
                    last.then_inc(lang_made, 1)
                    dve.wait_ge(grav_exp_made, b_count)
                    for ct in range(CT):
                        last = nc.vector.scalar_tensor_tensor(
                            out=grav[:, ct, :], in0=grav[:, ct, :], scalar=1.0, in1=adj_off[:, ct, :],
                            op0=ALU.min, op1=ALU.mult, accum_out=deg[:, 2 + ct:3 + ct])
                    last.then_inc(grav_made, 1)

                if opens(i):
                    for n, d in enumerate(FOLD_ORDER):
                        dve.wait_ge(wvo_hi_made, n + 1)
                        low_part(wvo_lo[:, d, :], bank[:, 4 + d, :], wvo_hi[:, d, :], wvo_split)

            turns(dve, turn)

        @block.tensor
        def _(pe):
            def turned(dst, src, done=None):
                last = nc.tensor.transpose(dst, src, ident[:])
                if done is not None:
                    last.then_inc(done, 1)

            pe.wait_ge(ident_made, 2)
            pe.wait_ge(consts_made, 2)
            pe.wait_ge(adj_loaded, 16)
            for c in range(CT):
                for o in range(CT):
                    turned(bank[:, 7, (c * CT + o) * P:(c * CT + o + 1) * P], adj_rows[:, o, c * P:(c + 1) * P],
                           adj_turned if c == o == CT - 1 else None)
            pe.wait_ge(adj_lo_made, 2)

            def triangle(k, first, last_d):
                pe.wait_ge(w_lo_made[k], 2)
                if k == 1:
                    for h in range(2):
                        pe.wait_ge(ah_split[h], 1)
                for d in range(first, last_d):
                    last = product(tri_place(k, d),
                                   [((w_hi[k][:, t, d * P:(d + 1) * P], w_lo[k][:, t, d * P:(d + 1) * P]),
                                     (w_hi[k][:, t, 0:TRI[d]], w_lo[k][:, t, 0:TRI[d]])) for t in range(DT)])
                if last_d == DT:
                    last.then_inc(tri_ready[k], 1)

            def turn_w_o():
                pe.wait_ge(tri_split[1], 1)
                pe.wait_ge(r_rows_copied, 1)
                pe.wait_ge(w_loaded[3], 32)
                for t in range(DT):
                    for e in range(DT):
                        turned(bank[:, t, e * P:(e + 1) * P], w_slot[1][e // 2][:, e % 2, t * P:(t + 1) * P],
                               wo_turned if e == DT - 1 else None)

            def fold_weights():
                pe.wait_ge(w_lo_made[2], 2)
                pe.wait_ge(wo_split, DT)
                for n, d in enumerate(FOLD_ORDER):
                    if n == 1:
                        pe.wait_ge(inv_sum_made, 1)
                    if n == 2:
                        pe.wait_ge(msg_scaled[0], 1)
                        pe.wait_ge(msg_scaled[1], 1)
                    product(bank[:, 4 + d, :],
                            [((w_hi[0][:, t, d * P:(d + 1) * P], w_lo[0][:, t, d * P:(d + 1) * P]),
                              (w_o_hi[t // 2][:, t % 2, :], w_o_lo[t // 2][:, t % 2, :])) for t in range(DT)]).then_inc(wvo_ready, 1)

            def turn(i, half):
                has_k, has_b, has_a, _ = which(i, half)
                k_count, b_count, a_count = i + half, i + (half + 1), i + (half + 2)
                def features(h):
                    for n in range(2 * h, 2 * h + 2):
                        nodes = slice(n * P, (n + 1) * P)
                        last = product(bank[:, n, 0:C + 2],
                                       [((h1_hi[:, c, nodes], h1_lo[:, c, nodes]),
                                         (adj_t_hi[:, c, :], adj_t_lo[:, c, :])) for c in range(CT)])
                    last.then_inc(ah_ready[h], 1)

                def tri_product(k, e, first=None, last_d=DT):
                    h, s = e // 2, e % 2
                    first = e if first is None else first
                    last = product(bank[:, 4 + 2 * k + h, s * C:(s + 1) * C],
                                   [((tri_hi[:, k, d, e * P:(e + 1) * P], tri_lo[:, k, d, e * P:(e + 1) * P]),
                                     (ht_hi[:, d, :], ht_lo[:, d, :])) for d in range(first, last_d)],
                                   begins=first == e, ends=last_d == DT)
                    if s == 0 and last_d == DT:
                        last.then_inc(t_ready[k][h], 1)

                def spread(dst, diagonals):
                    nc.tensor.matmul(dst, ones[:], diagonals[:, 4:8, :].rearrange("p t n -> p (t n)"),
                                     start=True, stop=False)
                    return nc.tensor.matmul(dst, ones[:], diagonals[:, 0:4, :].rearrange("p t n -> p (t n)"),
                                            start=False, stop=True)

                def y_product(k, t, first, last_e):
                    nodes = slice(t * P, (t + 1) * P)
                    last = product(bank[:, 1 + k, t * C:(t + 1) * C],
                                   [((t_hi[:, k, e, nodes], t_lo[:, k, e, nodes]),
                                     (ht_hi[:, e, :], ht_lo[:, e, :])) for e in range(first, last_e)],
                                   begins=first == 0, ends=last_e == DT)
                    if t == CT - 1 and last_e == DT:
                        last.then_inc(y_ready[k], 1)

                def turn_y(k):
                    pe.wait_ge(ys_copied[k], b_count)
                    for t in range(CT):
                        for s in range(CT):
                            turned(bank[:, 3 + k, (t * CT + s) * P:(t * CT + s + 1) * P],
                                   ys[:, k, s, t * P:(t + 1) * P], yt_ready[k] if t == s == CT - 1 else None)

                def messages(ct, first, last):
                    outs = slice(ct * P, (ct + 1) * P)
                    return product(bank[:, 5 + ct, :],
                                   [((ah_hi[:, n, outs], ah_lo[:, n, outs]),
                                     (att_hi[:, n, :], att_lo[:, n, :])) for n in range(first, last)],
                                   begins=first == 0, ends=last == DT)

                if has_a:
                    pe.wait_ge(h1_split, a_count)
                    if has_k:
                        pe.wait_ge(relu_made, k_count)
                        pe.wait_ge(u_copied[0], k_count)
                    features(0)
                if has_b:
                    pe.wait_ge(normed_made, b_count)
                    if isinstance(i, int) and i + half == 0:
                        pe.wait_ge(wvo_split, DT)
                    for h in (1, 0):
                        for s in range(2):
                            d = 2 * h + s
                            for t in range(CT):
                                turned(bank[:, 4 + 3 * h, (s * CT + t) * P:(s * CT + t + 1) * P],
                                       normed[:, t, d * P:(d + 1) * P], ht_ready[h] if s == t == 1 else None)
                if has_a:
                    if has_k:
                        pe.wait_ge(u_copied[1], k_count)
                    features(1)
                if opens(i):
                    triangle(0, 0, DT - 1)
                if has_b:
                    pe.wait_ge(ht_split[1], b_count)
                    tri_product(0, 3)
                    tri_product(0, 2)
                    pe.wait_ge(ht_split[0], b_count)
                    tri_product(0, 1)
                    tri_product(0, 0, 0, DT - 1)
                if has_k:
                    pe.wait_ge(k_made, k_count)
                    for t in range(CT):
                        for s in range(CT):
                            turned(bank[:, 6, (t * CT + s) * P:(t * CT + s + 1) * P],
                                   lang[:, s, t * P:(t + 1) * P], kt_ready if t == s == CT - 1 else None)
                if has_b:
                    tri_product(0, 0, DT - 1, DT)
                    tri_product(1, 3)
                    tri_product(1, 2)
                if has_a:
                    pe.wait_ge(r_diag_made, a_count)
                    pe.wait_ge(ah_split[1], a_count)
                    spread(bank[:, 2, :], r_diag).then_inc(r_rows_ready, 1)
                if opens(i):
                    triangle(0, DT - 1, DT)
                    triangle(1, 0, DT)
                k_late = has_k and has_b and not has_a

                def k_product():
                    pe.wait_ge(kt_split, k_count)
                    pe.wait_ge(u_split[1], k_count)
                    if has_a:
                        pe.wait_ge(ah_split[0], a_count)
                    for t in range(CT):
                        nodes = slice(t * P, (t + 1) * P)
                        product(bank[:, t, :],
                                [((kt_hi[:, m, nodes], kt_lo[:, m, nodes]),
                                  (u_hi[:, m, :], u_lo[:, m, :])) for m in range(CT)]).then_inc(agg_ready[t], 1)

                if has_k and not k_late:
                    k_product()
                if has_b:
                    if k_late:
                        pe.wait_ge(kt_split, k_count)
                    tri_product(1, 1)
                    tri_product(1, 0)
                    for h in range(2):
                        pe.wait_ge(t_split[0][h], b_count)
                    if has_k and not k_late:
                        pe.wait_ge(out_made[1], k_count)
                    for t in range(CT):
                        y_product(0, t, 0, DT)
                    pe.wait_ge(t_split[1][1], b_count)
                    pe.wait_ge(t_split[1][0], b_count)
                    if has_a:
                        pe.wait_ge(r_rows_copied, a_count)
                    y_product(1, 0, 0, 1)
                    if not has_k:
                        y_product(1, 0, 1, DT)
                        y_product(1, 1, 0, DT)
                if has_a:
                    pe.wait_ge(sum_split, a_count)
                    nc.tensor.matmul(bank[:, 7, :], ones[:], sum_lo[:], start=True, stop=False)
                    nc.tensor.matmul(bank[:, 7, :], ones[:], sum_hi[:], start=False, stop=True).then_inc(sum_ready, 1)
                if has_b:
                    if has_k:
                        y_product(1, 0, 1, DT)
                        y_product(1, 1, 0, DT)
                    turn_y(0)
                if opens(i):
                    pe.wait_ge(tri_split[0], 1)
                if has_a:
                    pe.wait_ge(att_split[0], a_count)
                    messages(0, 0, 1)
                if has_b:
                    turn_y(1)
                if k_late:
                    k_product()
                if has_a:
                    pe.wait_ge(att_split[1], a_count)
                    pe.wait_ge(att_tail_split, a_count)
                    messages(0, 1, DT).then_inc(msg_ready[0], 1)
                    if opens(i):
                        turn_w_o()
                    messages(1, 0, DT).then_inc(msg_ready[1], 1)
                if has_b:
                    def mixed_nodes(t):
                        nodes = slice(t * P, (t + 1) * P)
                        product(bank[:, 1 + t, :],
                                [((ht_hi[:, d, nodes], ht_lo[:, d, nodes]),
                                  (wvo_hi[:, d, :], wvo_lo[:, d, :])) for d in range(DT)]).then_inc(u_ready[t], 1)

                    if k_late:
                        for t in range(CT):
                            pe.wait_ge(out_made[t], k_count)
                    for part in range(2):
                        pe.wait_ge(row_diag_made[part], b_count)
                    spread(bank[:, 0, :], diag).then_inc(rows_ready, 1)
                    for t in range(CT):
                        mixed_nodes(t)

                if opens(i):
                    fold_weights()

            turns(pe, turn)


_INS = ["x", "adj", "L0_gnn_wq", "L0_gnn_wk", "L0_gnn_bm", "L1_gnn_W_lang", "L1_gnn_W_grav", "L1_gnn_W_V",
        "L1_gnn_W_O", "L1_gnn_gate_logit", "L1_gnn_log_sigma"]


def kernel(**inputs):
    import numpy as _np
    import concourse.bacc as _bacc
    from concourse import mybir as _mybir
    from concourse.bass_utils import run_bass_kernel_spmd as _run

    nc = _bacc.Bacc("TRN2", target_bir_lowering=False, num_devices=1)
    arrays, args = {}, []
    for name in _INS:
        a = _np.ascontiguousarray(inputs[name])
        if a.ndim == 0:
            a = a.reshape(1)
        arrays[f"in_{name}"] = a
        args.append(nc.dram_tensor(f"in_{name}", a.shape, _mybir.dt.from_np(a.dtype), kind="ExternalInput").ap())
    shape = inputs["x"].shape
    args.append(nc.dram_tensor("out_x", shape, _mybir.dt.float32, kind="ExternalOutput").ap())
    program(nc, *args)
    r = _run(nc, [arrays], core_ids=[0])
    return r.results[0]["out_x"]
```
